# Optimizing a Trainium2 kernel written in Bass

```python
import numpy as np
import jax
import jax.numpy as jnp

def _softmax(x, axis=-1):
    return jax.nn.softmax(x, axis=axis)

def _gelu(x):
    return jax.nn.gelu(x, approximate=True)

def _silu(x):
    return jax.nn.silu(x)

def _sigmoid(x):
    return jax.nn.sigmoid(x)

def _layernorm(x, axis=-1, eps=1e-05):
    m = jnp.mean(x, axis=axis, keepdims=True)
    v = jnp.var(x, axis=axis, keepdims=True)
    return (x - m) / jnp.sqrt(v + eps)

def _scatter_add(tgt, idx, src, axis=0):
    return tgt.at[idx].add(src)

def _segment_sum(src, seg, n):
    return jax.ops.segment_sum(src, seg, n)
kernel_name = 'mk_audio_tower_d1_tok_audfeat512_r4_6a5901'

def setup_inputs(seed: int=0):
    np.random.seed(seed)
    _w = jnp.asarray

    def _rec_inputs():
        import jax
        import jax.numpy as jnp
        _rk = jax.random.key(seed)
        x = 7.22013e-05 + 1.00017 * jax.random.normal(jax.random.fold_in(_rk, 1), (64, 750, 32), jnp.float32)
        return x
    x = _rec_inputs()

    def _L0_tok_setup():
        import jax, jax.numpy as jnp
        import numpy as np
        PATCH_LEN = 16
        PATCH_STRIDE = 8
        D_MODEL = 128
        N_FEATURES = 32
        key = jax.random.key(seed)
        k_x, k_w, k_b = jax.random.split(key, 3)
        x = jax.random.normal(k_x, (64, 1024, N_FEATURES), dtype=jnp.float32)
        in_dim = PATCH_LEN * N_FEATURES
        bound = 1.0 / np.sqrt(in_dim)
        W = jax.random.uniform(k_w, (D_MODEL, in_dim), dtype=jnp.float32, minval=-bound, maxval=bound)
        b = jax.random.uniform(k_b, (D_MODEL,), dtype=jnp.float32, minval=-bound, maxval=bound)
        return {'x': x, 'W': W, 'b': b}
    _L0_tok_all = _L0_tok_setup()
    _L0_tok_in = {k: v for k, v in _L0_tok_all.items() if k in ('W', 'b')}
    del _L0_tok_all

    def _L0_attn_setup():
        import jax, jax.numpy as jnp
        import numpy as np
        DIM = 128
        HEADS = 8
        DIM_HEAD = 64
        INNER = HEADS * DIM_HEAD
        LN_EPS = 1e-05
        key = jax.random.key(seed)
        ks = jax.random.split(key, 6)
        b, n = (2, 512)
        x = jax.random.normal(ks[0], (b, n, DIM), dtype=jnp.float32)
        w_qkv = jax.random.normal(ks[1], (3 * INNER, DIM), dtype=jnp.float32) * DIM ** (-0.5)
        reattn_w = jax.random.normal(ks[2], (HEADS, HEADS), dtype=jnp.float32)
        ln_g = jnp.ones((HEADS,), dtype=jnp.float32)
        ln_b = jnp.zeros((HEADS,), dtype=jnp.float32)
        w_out = jax.random.normal(ks[3], (DIM, INNER), dtype=jnp.float32) * INNER ** (-0.5)
        b_out = jnp.zeros((DIM,), dtype=jnp.float32)
        return {'x': x, 'w_qkv': w_qkv, 'reattn_w': reattn_w, 'ln_g': ln_g, 'ln_b': ln_b, 'w_out': w_out, 'b_out': b_out}
    _L0_attn_all = _L0_attn_setup()
    _L0_attn_in = {k: v for k, v in _L0_attn_all.items() if k in ('w_qkv', 'reattn_w', 'ln_g', 'ln_b', 'w_out', 'b_out')}
    del _L0_attn_all

    def _L0_ffn_setup():
        import jax, jax.numpy as jnp
        import numpy as np
        B, S, H, E, K, DF, SH = (8, 1024, 128, 8, 2, 128, 128)
        key = jax.random.key(seed)
        ks = jax.random.split(key, 10)
        n = lambda i, shape, sc: jax.random.normal(ks[i], shape, jnp.float32) * sc
        return {'hidden_states': n(0, (B, S, H), 1.0), 'gate_w': n(1, (E, H), 0.05), 'w1': n(2, (E, H, DF), 0.05), 'b1': n(3, (E, DF), 0.01), 'w2': n(4, (E, DF, H), 0.05), 'b2': n(5, (E, H), 0.01), 'sw1': n(6, (H, SH), 0.05), 'sb1': n(7, (SH,), 0.01), 'sw2': n(8, (SH, H), 0.05), 'sb2': n(9, (H,), 0.01)}
    _L0_ffn_all = _L0_ffn_setup()
    _L0_ffn_in = {k: v for k, v in _L0_ffn_all.items() if k in ('gate_w', 'w1', 'b1', 'w2', 'b2', 'sw1', 'sb1', 'sw2', 'sb2')}
    del _L0_ffn_all
    return {'x': x, 'L0_tok_W': _L0_tok_in['W'], 'L0_tok_b': _L0_tok_in['b'], 'L0_attn_w_qkv': _L0_attn_in['w_qkv'], 'L0_attn_reattn_w': _L0_attn_in['reattn_w'], 'L0_attn_ln_g': _L0_attn_in['ln_g'], 'L0_attn_ln_b': _L0_attn_in['ln_b'], 'L0_attn_w_out': _L0_attn_in['w_out'], 'L0_attn_b_out': _L0_attn_in['b_out'], 'L0_ffn_gate_w': _L0_ffn_in['gate_w'], 'L0_ffn_w1': _L0_ffn_in['w1'], 'L0_ffn_b1': _L0_ffn_in['b1'], 'L0_ffn_w2': _L0_ffn_in['w2'], 'L0_ffn_b2': _L0_ffn_in['b2'], 'L0_ffn_sw1': _L0_ffn_in['sw1'], 'L0_ffn_sb1': _L0_ffn_in['sb1'], 'L0_ffn_sw2': _L0_ffn_in['sw2'], 'L0_ffn_sb2': _L0_ffn_in['sb2']}

def reference(x, L0_tok_W, L0_tok_b, L0_attn_w_qkv, L0_attn_reattn_w, L0_attn_ln_g, L0_attn_ln_b, L0_attn_w_out, L0_attn_b_out, L0_ffn_gate_w, L0_ffn_w1, L0_ffn_b1, L0_ffn_w2, L0_ffn_b2, L0_ffn_sw1, L0_ffn_sb1, L0_ffn_sw2, L0_ffn_sb2):
    import jax
    import jax.numpy as jnp

    def _L0_tok_ref(x, W, b):
        import jax, jax.numpy as jnp
        import numpy as np
        PATCH_LEN = 16
        PATCH_STRIDE = 8
        D_MODEL = 128
        N_FEATURES = 32
        B, T, C = x.shape
        n_patches = (T - PATCH_LEN) // PATCH_STRIDE + 1
        idx = jnp.arange(n_patches)[:, None] * PATCH_STRIDE + jnp.arange(PATCH_LEN)[None, :]
        patches = x[:, idx, :]
        patches = patches.reshape(B, n_patches, PATCH_LEN * C)
        return jnp.einsum('bpf,df->bpd', patches, W) + b

    def _L0_attn_ref(x, w_qkv, reattn_w, ln_g, ln_b, w_out, b_out):
        import jax, jax.numpy as jnp
        import numpy as np
        DIM = 128
        HEADS = 8
        DIM_HEAD = 64
        INNER = HEADS * DIM_HEAD
        LN_EPS = 1e-05
        b, n, _ = x.shape
        scale = DIM_HEAD ** (-0.5)
        qkv = x @ w_qkv.T
        q, k, v = jnp.split(qkv, 3, axis=-1)
        split_heads = lambda t: t.reshape(b, n, HEADS, DIM_HEAD).transpose(0, 2, 1, 3)
        q, k, v = (split_heads(q), split_heads(k), split_heads(v))
        dots = jnp.einsum('bhid,bhjd->bhij', q, k) * scale
        attn = jax.nn.softmax(dots, axis=-1)
        attn = jnp.einsum('bhij,hg->bgij', attn, reattn_w)
        a = attn.transpose(0, 2, 3, 1)
        mu = jnp.mean(a, axis=-1, keepdims=True)
        var = jnp.mean((a - mu) ** 2, axis=-1, keepdims=True)
        a = (a - mu) * jax.lax.rsqrt(var + LN_EPS) * ln_g + ln_b
        attn = a.transpose(0, 3, 1, 2)
        out = jnp.einsum('bhij,bhjd->bhid', attn, v)
        out = out.transpose(0, 2, 1, 3).reshape(b, n, INNER)
        out = out @ w_out.T + b_out
        return out

    def _L0_ffn_ref(hidden_states, gate_w, w1, b1, w2, b2, sw1, sb1, sw2, sb2):
        import jax, jax.numpy as jnp
        import numpy as np
        B, S, H, E, K, DF, SH = (8, 1024, 128, 8, 2, 128, 128)
        x = hidden_states
        xf = x.reshape(-1, x.shape[-1])
        T = xf.shape[0]
        scores = jax.nn.softmax(xf @ gate_w.T, axis=-1)
        topk_w, topk_i = jax.lax.top_k(scores, K)
        topk_w = topk_w / (topk_w.sum(-1, keepdims=True) + 1e-20)
        combine = jnp.zeros((T, E), xf.dtype).at[jnp.arange(T)[:, None], topk_i].add(topk_w)
        h1 = jax.nn.relu(jnp.einsum('th,ehf->tef', xf, w1) + b1)
        eo = jnp.einsum('tef,efh->teh', h1, w2) + b2
        y = jnp.einsum('te,teh->th', combine, eo)
        shared = jax.nn.relu(xf @ sw1 + sb1) @ sw2 + sb2
        return (y + shared).reshape(x.shape)
    h = _L0_tok_ref(x, L0_tok_W, L0_tok_b)
    h = h + _L0_attn_ref(_layernorm(h, axis=-1), L0_attn_w_qkv, L0_attn_reattn_w, L0_attn_ln_g, L0_attn_ln_b, L0_attn_w_out, L0_attn_b_out)
    h = h + _L0_ffn_ref(_layernorm(h, axis=-1), L0_ffn_gate_w, L0_ffn_w1, L0_ffn_b1, L0_ffn_w2, L0_ffn_b2, L0_ffn_sw1, L0_ffn_sb1, L0_ffn_sw2, L0_ffn_sb2)
    return h

_drawn_inputs = setup_inputs


def setup_inputs(seed=0):
    import zlib

    import numpy as np

    out = dict(_drawn_inputs(seed))
    spreads = {'L0_attn_ln_g': (1.0, 0.2), 'L0_attn_ln_b': (0.0, 0.1), 'L0_attn_b_out': (0.0, 0.8)}
    factors = {'L0_ffn_gate_w': 5.303,
     'L0_ffn_w1': 5.563,
     'L0_ffn_b1': 54.571,
     'L0_ffn_w2': 4.56,
     'L0_ffn_b2': 64.0,
     'L0_ffn_sw1': 4.157,
     'L0_ffn_sb1': 60.003,
     'L0_ffn_sw2': 3.426,
     'L0_ffn_sb2': 64.0}
    for name, (base, spread) in spreads.items():
        noise = np.random.default_rng([zlib.crc32(name.encode()), seed]).standard_normal(out[name].shape)
        drawn = base * np.exp(spread * noise) if base else spread * noise
        out[name] = jnp.asarray(drawn.astype(out[name].dtype))
    for name, factor in factors.items():
        out[name] = (out[name] * factor).astype(out[name].dtype)
    return out
```

```python
from contextlib import ExitStack

import numpy as np

import concourse.bass as bass
from concourse import mybir

F32 = mybir.dt.float32
ALU = mybir.AluOpType
ACT = mybir.ActivationFunctionType
AX_X = mybir.AxisListType.X

B, T, C = 64, 750, 32
PATCH, STRIDE = 16, 8
D = 128
N = (T - PATCH) // STRIDE + 1
HEADS, DH = 8, 64
E = 8
SLOTS = 4
NG = B // SLOTS
W = SLOTS * N
PAIRS = STRIDE * C
NP2 = N + 1
KT = PATCH * C // D
IC = 16
CHUNKS = 6
STARTS = [0, 15, 30, 46, 61, 76]
HALF = CHUNKS // 2
LN_EPS = 1e-5
N_ROUTE = 18

BEHIND = {"dots": 0, "inv": 0, "mix": 1, "rstd": 1, "scale": 1, "av": 2}
SCHEDULE = [
    [("dots", 0), "Z0", "C0", "Z1", "C1", ("mix", 0), "Z2", "C2", "Z3", "C3", ("av", 0), ("inv", 0), "Z4",
     ("rstd", 0), "C4", ("scale", 0)],
    [("dots", 1), "Z5", "C5", "Z6", "C6", ("mix", 1), "Z7", "C7", "Z8", ("av", 1), ("inv", 1), "XE", "XO",
     ("rstd", 1), "YF", ("scale", 1)],
    [("dots", 2), "V2", "OP", "shift", ("mix", 2), "TK", "OT", "TH2", ("av", 2), ("inv", 2), "TH", ("rstd", 2), "V3",
     ("scale", 2)],
    [("dots", 3), "TX2", "TX", ("mix", 3), "RT", "Y0", "Y1", "Y2", "BS", ("av", 3), ("inv", 3), "Y3", "Y4", "CT",
     "Y5", ("rstd", 3), "Y6", "Y7", "V0", "V1", ("scale", 3)],
]
LAG = {"XE": 1, "XO": 1, "TK": 1, "TH": 1, "TX": 1, "BS": 1, "V0": 1, "V1": 1, "V2": 0, "V3": 0,
       "OP": -1, "TH2": -1, "TX2": -1, "RT": -1, "CT": -1, "YF": -2, "OT": -2, "shift": 0}
LAG.update({f"Y{h}": 1 for h in range(HEADS)})
LAG.update({f"Z{e}": -2 for e in range(E + 1)})
LAG.update({f"C{e}": -2 for e in range(E)})
STEPS = [step for slot in SCHEDULE for step in slot]
FILLS = [step for step in STEPS if isinstance(step, str) and step != "shift"]
PROLOGUE = ["pT", "pO", "pV", "pA0", "pA1", "pB", "pM"]
NBANK = 3
BANK = {step: n % NBANK for n, step in enumerate(FILLS)}
BANK.update({step: n % NBANK for n, step in enumerate(PROLOGUE)})
FIRST, STEADY, END = -1, 2, NG - 2
LAST = NG + 2


def exists(n, count):
    return not isinstance(n, int) or 0 <= n < count


def present(step, G):
    if isinstance(step, tuple):
        kind, s = step
        return exists(SLOTS * G + s - BEHIND[kind], B)
    return exists(G + LAG[step], NG)


def fills_before(step, G, more=0):
    if step in PROLOGUE:
        return more + sum(BANK[p] == BANK[step] for p in PROLOGUE[:PROLOGUE.index(step)])
    total = more + sum(BANK[p] == BANK[step] for p in PROLOGUE)
    same = [other for other in FILLS if BANK[other] == BANK[step]]
    ahead = [LAG[other] + (FILLS.index(other) < FILLS.index(step)) for other in same]
    if isinstance(G, int):
        return total + sum(max(0, min(NG, G + n)) for n in ahead)
    return G * len(same) + (total + sum(ahead))


def audio_tower(nc, x, tok_W, tok_b, w_qkv, reattn_w, ln_g, ln_b, w_out, b_out, gate_w, w1, b1, w2, b2,
                sw1, sb1, sw2, sb2, ident_dram, rev_dram, out):
    with ExitStack() as ctx:
        def sb(name, shape):
            return ctx.enter_context(nc.sbuf_tensor(name, shape, F32))

        def sem(name):
            return ctx.enter_context(nc.semaphore(name))

        ps_dots = ctx.enter_context(nc.psum_tensor("ps_dots", [128, 2, 512], F32))
        ps_mix = ctx.enter_context(nc.psum_tensor("ps_mix", [128, 2, 512], F32))
        ps_av = ctx.enter_context(nc.psum_tensor("ps_av", [128, 512], F32))
        ps_fill = [ctx.enter_context(nc.psum_tensor(f"ps_fill{k}", [128, 512], F32)) for k in range(NBANK)]

        ident = sb("ident", [128, 128])
        rev = sb("rev", [N, SLOTS, E])
        eps = sb("eps", [128, SLOTS])
        ones = sb("ones", [128, SLOTS])
        scratch = sb("scratch", [N, 1])
        minus_half = sb("minus_half", [128, SLOTS])
        qkv = sb("qkv", [128, 12, 128])
        tok_nat = sb("tok_nat", [128, KT, 128])
        wo_nat = sb("wo_nat", [128, 4, 128])
        vecs = sb("vecs", [12, 128])
        gate_nat = sb("gate_nat", [E, 128])
        b2_sb = sb("b2_sb", [E, 128])
        lng = sb("lng", [128, HEADS])
        lnb = sb("lnb", [128, HEADS])
        mixw = sb("mixw", [128, HEADS])
        mixmean = sb("mixmean", [128, 2])
        mixc = sb("mixc", [128, HEADS])
        diag16 = sb("diag16", [128, IC])
        mixk = sb("mixk", [128, HEADS, IC])
        tokT = sb("tokT", [128, KT, 128])
        woT = sb("woT", [128, 4, 128])
        woTb = sb("woTb", [128, 4, 128])
        wv_g = sb("wv_g", [128, 4, 128])
        wvT = sb("wvT", [128, 4, 128])
        A = sb("A", [128, HEADS, 128])
        M = sb("M", [128, 128])
        vecT = sb("vecT", [128, 32])
        w1_sb = sb("w1_sb", [128, E + 1, 128])
        w2_sb = sb("w2_sb", [128, E + 1, 128])

        xin = sb("xin", [NP2, SLOTS, PAIRS])
        xe = sb("xe", [128, SLOTS, NP2])
        xo = sb("xo", [128, SLOTS, NP2])
        hT = sb("hT", [128, SLOTS, N])
        hT_old = sb("hT_old", [128, SLOTS, N])
        stats = [sb(f"stats{k}", [N, SLOTS, 6]) for k in range(2)]
        mv = [sb(f"mv{k}", [N, SLOTS, 2]) for k in range(2)]
        vare = [sb(f"vare{k}", [N, SLOTS]) for k in range(2)]
        rstd = [sb(f"rstd{k}", [N, SLOTS]) for k in range(2)]
        xn = [sb(f"xn{k}", [N, SLOTS, 128]) for k in range(2)]
        xT = sb("xT", [128, SLOTS, N])
        xsum = sb("xsum", [128, SLOTS])
        bias = sb("bias", [128, SLOTS])
        bias_old = sb("bias_old", [128, SLOTS])
        yT = sb("yT", [128, 2 * SLOTS, HALF, HEADS, IC])
        v_sb = sb("v_sb", [N, SLOTS, HEADS * DH])

        negmax = sb("negmax", [128, CHUNKS])
        sums = sb("sums", [128, 2, CHUNKS])
        rinv = sb("rinv", [128, 2, CHUNKS])
        ex = sb("ex", [128, 2, CHUNKS, N])
        probs = sb("probs", [128, 2, CHUNKS, N])
        sq = sb("sq", [N, CHUNKS, HEADS, IC])
        sum4 = sb("sum4", [N, CHUNKS, 4, IC])
        sum2 = sb("sum2", [N, CHUNKS, 2, IC])
        sumsq = sb("sumsq", [N, CHUNKS, IC])
        lnvar = sb("lnvar", [N, CHUNKS, IC])
        arstd = sb("arstd", [N, CHUNKS, IC])
        aT = sb("aT", [N, 2, HEADS, N])
        oT = sb("oT", [128, HEADS // 2, SLOTS, N])

        h2T = sb("h2T", [128, SLOTS, N])
        x2T = sb("x2T", [128, W])
        logit = sb("logit", [N, SLOTS, E])
        shift_l = sb("shift_l", [N, SLOTS, E])
        exl = sb("exl", [N, SLOTS, E])
        key1 = sb("key1", [N, SLOTS, E])
        hot1 = sb("hot1", [N, SLOTS, E])
        rest = sb("rest", [N, SLOTS, E])
        key2 = sb("key2", [N, SLOTS, E])
        hot2 = sb("hot2", [N, SLOTS, E])
        top = sb("top", [N, 8, SLOTS])
        combine = sb("combine", [N, SLOTS, E])
        combT = sb("combT", [E, W])
        act1 = sb("act1", [128, E + 1, W])
        fT = sb("fT", [128, SLOTS, N])
        ostage = sb("ostage", [N, SLOTS, 128])

        filled = [sem(f"filled{k}") for k in range(NBANK)]
        emptied = [sem(f"emptied{k}") for k in range(NBANK)]
        consts_loaded = sem("consts_loaded")
        experts_loaded = sem("experts_loaded")
        pool_consts = sem("pool_consts")
        x_loaded = sem("x_loaded")
        stored = sem("stored")
        prep = sem("prep")
        dots_ready = sem("dots_ready")
        max_ready = sem("max_ready")
        exp_ready = sem("exp_ready")
        rinv_ready = sem("rinv_ready")
        probs_ready = sem("probs_ready")
        mix_ready = sem("mix_ready")
        sq_ready = sem("sq_ready")
        tree4 = sem("tree4")
        tree2 = sem("tree2")
        sumsq_ready = sem("sumsq_ready")
        lnvar_ready = sem("lnvar_ready")
        arstd_ready = sem("arstd_ready")
        aT_ready = sem("aT_ready")
        av_ready = sem("av_ready")
        oT_ready = sem("oT_ready")
        stats_ready = [sem(f"stats_ready{k}") for k in range(2)]
        mv_ready = [sem(f"mv_ready{k}") for k in range(2)]
        vare_ready = [sem(f"vare_ready{k}") for k in range(2)]
        rstd_ready = [sem(f"rstd_ready{k}") for k in range(2)]
        xsum_ready = sem("xsum_ready")
        shifted = sem("shifted")
        exl_ready = sem("exl_ready")
        route = sem("route")

        def at_least(eng, s, value):
            if isinstance(value, int) and value <= 0:
                return
            eng.wait_ge(s, value)

        def wait_filled(eng, step, G=0):
            at_least(eng, filled[BANK[step]], fills_before(step, G, 1))

        def wait_emptied(eng, step, G=0):
            if step in PROLOGUE or present(step, G):
                at_least(eng, emptied[BANK[step]], fills_before(step, G, 1))

        def wait_free(eng, step, G=0):
            at_least(eng, emptied[BANK[step]], fills_before(step, G))

        def chunked(ps):
            whole = ps[:, 0:W]
            return bass.AP(tensor=whole.tensor, offset=whole.offset,
                           ap=[list(whole.ap[0]), [STARTS[HALF], 2 * SLOTS], [STARTS[1], HALF], [1, IC]])

        def bank(step):
            return ps_fill[BANK[step]]

        def run(eng, do):
            def iteration(G):
                for step in STEPS:
                    if present(step, G):
                        do(step, G)

            for G in range(FIRST, STEADY):
                iteration(G)
            with eng.Fori(STEADY, END) as G:
                iteration(G)
            for G in range(END, LAST):
                iteration(G)

        x_rows = x.rearrange("b t c -> b (t c)")
        x_pairs = x_rows[:, 0:NP2 * PAIRS].rearrange("b (p k) -> p b k", p=NP2)
        out_rows = out.rearrange("b p d -> p b d")

        N_CONSTS = 22

        block = ctx.enter_context(nc.Block())

        @block.sync
        def _(sp):
            def load(g):
                sp.dma_start(xin[:, :, :], x_pairs[:, bass.ds(SLOTS * g, SLOTS), :]).then_inc(x_loaded, 16)

            consts = [
                (ident[:, :], ident_dram),
                (tok_nat[:, :, :], tok_W.rearrange("d (k f) -> d k f", k=KT)),
                (vecs[0:8, :], b1), (vecs[8:9, :], sb1.unsqueeze(0)), (vecs[9:10, :], sb2.unsqueeze(0)),
                (vecs[10:11, :], tok_b.unsqueeze(0)), (vecs[11:12, :], b_out.unsqueeze(0)),
                (qkv[:, :, :], w_qkv.rearrange("(c p) d -> p c d", p=128)),
                (wo_nat[:, :, :], w_out.rearrange("d (k f) -> d k f", k=4)),
                (gate_nat[:, :], gate_w), (b2_sb[:, :], b2),
                (rev[:, :, :], rev_dram),
            ]
            for dst, src in ((lng, ln_g), (lnb, ln_b)):
                consts.append((dst[:, :], bass.AP(tensor=src.tensor, offset=0, ap=[[0, 128], [1, HEADS]])))
            for h in range(HEADS):
                consts.append((mixw[IC * h:IC * h + IC, :],
                               bass.AP(tensor=reattn_w.tensor, offset=HEADS * h, ap=[[0, IC], [1, HEADS]])))
            assert len(consts) == N_CONSTS
            load(0)
            for dst, src in consts:
                sp.dma_start(dst, src).then_inc(consts_loaded, 16)
            sp.dma_start(w1_sb[:, 0:E, :], w1.rearrange("e h f -> h e f")).then_inc(experts_loaded, 16)
            sp.dma_start(w1_sb[:, E, :], sw1).then_inc(experts_loaded, 16)
            sp.dma_start(w2_sb[:, 0:E, :], w2.rearrange("e f h -> f e h")).then_inc(experts_loaded, 16)
            sp.dma_start(w2_sb[:, E, :], sw2).then_inc(experts_loaded, 16)

            def do(step, G):
                if step == "XO" and exists(G + 2, NG):
                    wait_filled(sp, "XO", G)
                    load(G + 2)
                if step == "OT":
                    wait_emptied(sp, "OT", G)
                    sp.dma_start(out_rows[:, bass.ds(SLOTS * (G - 2), SLOTS), :],
                                 ostage[:, :, :]).then_inc(stored, 16)

            run(sp, do)
            sp.wait_ge(stored, 16 * NG)

        @block.tensor
        def _(pe):
            def fill(step, G=0):
                wait_free(pe, step, G)
                return bank(step)

            def transposes(step, G, pieces):
                for o, i, d in pieces:
                    last = pe.transpose(o, i, d)
                last.then_inc(filled[BANK[step]], 1)

            pe.wait_ge(consts_loaded, 16 * N_CONSTS)
            ps = fill("pT")
            transposes("pT", 0, [(ps[:, 128 * k:128 * k + 128], tok_nat[:, k, :], ident[:, :]) for k in range(KT)])
            ps = fill("pO")
            transposes("pO", 0, [(ps[:, 128 * k:128 * k + 128], wo_nat[:, k, :], ident[:, :]) for k in range(4)])
            pe.wait_ge(prep, 1)
            ps = fill("pV")
            transposes("pV", 0, [(ps[:, 128 * k:128 * k + 128], wv_g[:, k, :], ident[:, :]) for k in range(4)])
            for half in range(2):
                step = f"pA{half}"
                ps = fill(step)
                rows = slice(DH * half, DH * half + DH)
                for k in range(4):
                    last = pe.matmul(ps[:, 128 * k:128 * k + 128], qkv[rows, k, :], qkv[rows, 4 + k, :],
                                     start=True, stop=True)
                last.then_inc(filled[BANK[step]], 1)
            ps = fill("pB")
            transposes("pB", 0, [(ps[:, 0:12], vecs[:, :], ident[0:12, 0:12]),
                                 (ps[:, 16:24], gate_nat[:, :], ident[0:E, 0:E])])
            ps = fill("pM")
            pe.wait_ge(prep, 2)
            for k in range(4):
                last = pe.matmul(ps[:, 0:128], qkv[:, 8 + k, :], woTb[:, k, :], start=(k == 0), stop=(k == 3))
            last.then_inc(filled[BANK["pM"]], 1)
            wait_emptied(pe, "pM")

            def attention(kind, b, s):
                if kind == "dots":
                    g = G_of[0]
                    wait_emptied(pe, "Y6", g - 1)
                    wait_emptied(pe, "Y7", g - 1)
                    at_least(pe, exp_ready, b)
                    for c in range(CHUNKS):
                        last = pe.matmul(ps_dots[:, c // HALF, N * (c % HALF):N * (c % HALF) + N],
                                         yT[:, 2 * s + c // HALF, c % HALF, :, :].rearrange("p h i -> p (h i)"), xT[:, s, :], start=True, stop=True)
                    last.then_inc(dots_ready, 1)
                elif kind == "mix":
                    pe.wait_ge(probs_ready, b + 1)
                    at_least(pe, aT_ready, b)
                    for c in range(CHUNKS):
                        o = 128 * (c % HALF)
                        last = pe.matmul(ps_mix[0:N, c // HALF, o:o + 128], probs[:, (s - 1) % 2, c, :],
                                         mixk[:, :, :].rearrange("p g i -> p (g i)"), start=True, stop=True)
                    last.then_inc(mix_ready, 1)
                else:
                    pe.wait_ge(aT_ready, b + 1)
                    at_least(pe, oT_ready, b)
                    for g in range(HEADS):
                        o = DH * (g % 2)
                        last = pe.matmul(ps_av[o:o + DH, N * (g // 2):N * (g // 2) + N],
                                         v_sb[:, (s - 2) % SLOTS, DH * g:DH * g + DH], aT[:, s % 2, g, :],
                                         start=True, stop=True)
                    last.then_inc(av_ready, 1)

            G_of = [0]

            def do(step, G):
                if isinstance(step, tuple):
                    kind, s = step
                    G_of[0] = G
                    if kind == "av":
                        vs = (s - 2) % SLOTS
                        wait_emptied(pe, f"V{vs}", G - 1)
                    if kind in ("dots", "mix", "av"):
                        attention(kind, SLOTS * G + s - BEHIND[kind], s)
                    return
                if step == "shift":
                    return
                g = G + LAG[step]
                if step == "XE":
                    pe.wait_ge(x_loaded, 16 * g + 16)
                if step == "TK":
                    wait_emptied(pe, "XE", G)
                    wait_emptied(pe, "XO", G)
                if step == "TH":
                    wait_emptied(pe, "TK", G)
                if step == "TH2":
                    wait_emptied(pe, "OP", G)
                if step == "TX":
                    wait_emptied(pe, "TH", G)
                if step == "TX2":
                    wait_emptied(pe, "TH2", G)
                if step == "Y0":
                    wait_emptied(pe, "TX", G)
                if step == "RT":
                    wait_emptied(pe, "TX2", G)
                if step == "BS":
                    pe.wait_ge(xsum_ready, g + 1)
                if step == "OP":
                    pe.wait_ge(oT_ready, SLOTS * g + SLOTS)
                if step in ("CT", "C0"):
                    pe.wait_ge(route, N_ROUTE * (g + 1))
                if step == "RT" and isinstance(G, int):
                    pe.wait_ge(experts_loaded, 64)
                if step == "YF":
                    wait_emptied(pe, f"C{E - 1}", G)
                    wait_emptied(pe, "Z8", G)
                    wait_emptied(pe, "CT", G - 1)
                if step == "OT":
                    wait_emptied(pe, "YF", G)
                ps = fill(step, G)
                done = filled[BANK[step]]
                if step in ("XE", "XO"):
                    odd = 128 * (step == "XO")
                    transposes(step, G, [(ps[:, NP2 * s:NP2 * s + NP2], xin[:, s, odd:odd + 128],
                                          ident[0:NP2, 0:NP2]) for s in range(SLOTS)])
                elif step == "TK":
                    for k in range(KT):
                        rows = (xe, xo)[k % 2][:, :, k // 2:k // 2 + N]
                        last = pe.matmul(ps[:, 0:W], tokT[:, k, :], rows, start=(k == 0), stop=(k == KT - 1))
                    last.then_inc(done, 1)
                elif step in ("TH", "TH2"):
                    src = hT if step == "TH" else h2T
                    transposes(step, G, [(ps[0:N, 128 * s:128 * s + 128], src[:, s, :], ident[:, :])
                                         for s in range(SLOTS)])
                elif step in ("TX", "TX2"):
                    src = xn[step == "TX2"]
                    transposes(step, G, [(ps[:, N * s:N * s + N], src[:, s, :], ident[0:N, 0:N])
                                         for s in range(SLOTS)])
                elif step[0] == "Y" and step != "YF":
                    pe.matmul(ps[:, 0:W], A[:, int(step[1]), :], xT[:, :, :], start=True, stop=True).then_inc(done, 1)
                elif step[0] == "V":
                    pe.matmul(ps[0:N, :], xT[:, int(step[1]), :], wvT[:, :, :], start=True, stop=True)\
                      .then_inc(done, 1)
                elif step == "BS":
                    pe.matmul(ps[:, 0:SLOTS], M[:, :], xsum[:, :], start=True, stop=True).then_inc(done, 1)
                elif step == "OP":
                    for k in range(4):
                        last = pe.matmul(ps[:, 0:W], woT[:, k, :], oT[:, k, :, :], start=(k == 0), stop=(k == 3))
                    last.then_inc(done, 1)
                elif step == "RT":
                    for s in range(SLOTS):
                        last = pe.matmul(ps[0:N, E * s:E * s + E], x2T[:, N * s:N * s + N], vecT[:, 16:16 + E],
                                         start=True, stop=True)
                    last.then_inc(done, 1)
                elif step == "CT":
                    transposes(step, G, [(ps[0:E, N * s:N * s + N], combine[:, s, :], ident[0:N, 0:N])
                                         for s in range(SLOTS)])
                elif step[0] == "Z":
                    pe.matmul(ps[:, 0:W], w1_sb[:, int(step[1]), :], x2T[:, :], start=True, stop=True)\
                      .then_inc(done, 1)
                elif step[0] == "C":
                    e = int(step[1])
                    transposes(step, G, [(ps[:, N * s:N * s + N],
                                          combine[:, s, e:e + 1].broadcast_to([N, 128]), ident[0:N, 0:N])
                                         for s in range(SLOTS)])
                elif step == "YF":
                    pe.matmul(ps[:, 0:W], b2_sb[:, :], combT[:, :], start=True, stop=False)
                    for e in range(E + 1):
                        last = pe.matmul(ps[:, 0:W], w2_sb[:, e, :], act1[:, e, :], start=False, stop=(e == E))
                    last.then_inc(done, 1)
                elif step == "OT":
                    transposes(step, G, [(ps[0:N, 128 * s:128 * s + 128], fT[:, s, :], ident[:, :])
                                         for s in range(SLOTS)])

            run(pe, do)

        @block.scalar
        def _(act):
            def empty(step, G, dst, src, **kw):
                wait_filled(act, step, G)
                act.activation(dst, src, kw.pop("func", ACT.Copy), **kw).then_inc(emptied[BANK[step]], 1)

            def softmax_exp(b, s):
                act.wait_ge(max_ready, b + 1)
                at_least(act, probs_ready, b - 1)
                for c in range(CHUNKS):
                    last = act.activation(ex[:, s % 2, c, :], ps_dots[:, c // HALF, N * (c % HALF):N * (c % HALF) + N],
                                          ACT.Exp, bias=negmax[:, c:c + 1], accum_out=sums[:, s % 2, c:c + 1])
                last.then_inc(exp_ready, 1)

            def square(b):
                act.wait_ge(mix_ready, b + 1)
                at_least(act, sumsq_ready, b)
                act.activation(sq[:, :, :, :].rearrange("p (a c) g i -> p a (c g i)", a=2),
                               ps_mix[0:N, :, 0:128 * HALF], ACT.Square).then_inc(sq_ready, 1)

            def attention_rstd(b):
                act.wait_ge(sumsq_ready, b + 1)
                act.activation(lnvar[:, :, :], sumsq[:, :, :], ACT.Ln, bias=eps[0:N, 0:1], scale=1.0 / HEADS)\
                   .then_inc(lnvar_ready, 1)
                at_least(act, aT_ready, b)
                act.wait_ge(lnvar_ready, b + 1)
                act.activation(arstd[:, :, :], lnvar[:, :, :], ACT.Exp, scale=-0.5).then_inc(arstd_ready, 1)

            act.wait_ge(pool_consts, 1)
            wait_emptied(act, "pM")

            def do(step, G):
                if isinstance(step, tuple):
                    kind, s = step
                    b = SLOTS * G + s - BEHIND[kind]
                    if kind == "dots":
                        softmax_exp(b, s)
                    if kind == "mix":
                        square(b)
                    if kind == "rstd":
                        attention_rstd(b)
                    return
                if step == "shift":
                    return
                g = G + LAG[step]
                ps = bank(step)
                if step in ("XE", "XO"):
                    empty(step, G, (xe if step == "XE" else xo)[:, :, :].rearrange("p s n -> p (s n)"),
                          ps[:, 0:SLOTS * NP2])
                elif step == "TK":
                    at_least(act, shifted, G + 1)
                    empty(step, G, hT[:, :, :].rearrange("p s n -> p (s n)"), ps[:, 0:W], func=ACT.Identity,
                          bias=vecT[:, 10:11])
                elif step == "TX":
                    wait_emptied(act, "BS", G - 1)
                    empty(step, G, xT[:, :, :].rearrange("p s n -> p (s n)"), ps[:, 0:W])
                elif step == "TX2":
                    empty(step, G, x2T[:, :], ps[:, 0:W])
                elif step in ("Y0", "Y2", "Y4", "Y6"):
                    empty(step, G, yT[:, :, :, int(step[1]), :], chunked(ps))
                elif step in ("V0", "V2", "V3"):
                    empty(step, G, v_sb[:, int(step[1]), :], ps[0:N, :])
                elif step == "RT":
                    act.wait_ge(route, N_ROUTE * g + 2)
                    act.activation(exl[:, :, :], shift_l[:, :, :], ACT.Exp).then_inc(exl_ready, 1)
                elif step[0] == "Z":
                    e = int(step[1])
                    if e == 0:
                        wait_filled(act, "YF", G - 1) if present("YF", G - 1) else None
                    wait_filled(act, step, G)
                    ins = act.activation(act1[:, e, :], ps[:, 0:W], ACT.Relu, bias=vecT[:, e:e + 1])
                    ins.then_inc(emptied[BANK[step]], 1)
                elif step == "OT":
                    at_least(act, stored, 16 * g)
                    empty(step, G, ostage[:, :, :].rearrange("p s n -> p (s n)"), ps[0:N, :])

            run(act, do)

        @block.vector
        def _(dve):
            def empty(step, G, dst, src):
                wait_filled(dve, step, G)
                dve.tensor_copy(dst, src).then_inc(emptied[BANK[step]], 1)

            dve.wait_ge(consts_loaded, 16 * N_CONSTS)
            for half in range(2):
                rows = slice(DH * half, DH * half + DH)
                last = dve.tensor_tensor(wv_g[rows, :, :], qkv[rows, 8:12, :],
                                         lng[rows, half::2].unsqueeze(2).broadcast_to([DH, 4, 128]), ALU.mult)
            last.then_inc(prep, 1)
            empty("pT", 0, tokT[:, :, :].rearrange("p k m -> p (k m)"), bank("pT")[:, :])
            empty("pO", 0, woT[:, :, :].rearrange("p k m -> p (k m)"), bank("pO")[:, :])
            wait_emptied(dve, "pO")
            for half in range(2):
                rows = slice(DH * half, DH * half + DH)
                last = dve.tensor_tensor(woTb[rows, :, :], woT[rows, :, :],
                                         lnb[rows, half::2].unsqueeze(2).broadcast_to([DH, 4, 128]), ALU.mult)
            last.then_inc(prep, 1)
            empty("pV", 0, wvT[:, :, :].rearrange("p k m -> p (k m)"), bank("pV")[:, :])
            for half in range(2):
                step = f"pA{half}"
                wait_filled(dve, step)
                dve.tensor_scalar(A[:, half::2, :], bank(step)[:, :].rearrange("p (k m) -> p k m", k=4),
                                  float(DH) ** -0.5, None, ALU.mult).then_inc(emptied[BANK[step]], 1)
            wait_filled(dve, "pB")
            dve.tensor_copy(vecT[:, 0:12], bank("pB")[:, 0:12])
            dve.tensor_copy(vecT[:, 16:24], bank("pB")[:, 16:24]).then_inc(emptied[BANK["pB"]], 1)
            dve.tensor_reduce(mixmean[:, 0:1], mixw[:, :], AX_X, ALU.add).then_inc(prep, 1)
            dve.tensor_reduce(diag16[:, :], ident[:, :].rearrange("p (h i) -> p i h", i=IC), AX_X, ALU.add)\
               .then_inc(prep, 1)
            dve.wait_ge(prep, 4)
            dve.tensor_scalar(mixmean[:, 1:2], mixmean[:, 0:1], 1.0 / HEADS, None, ALU.mult).then_inc(prep, 1)
            dve.wait_ge(prep, 5)
            dve.tensor_scalar(mixc[:, :], mixw[:, :], mixmean[:, 1:2], None, ALU.subtract).then_inc(prep, 1)
            dve.wait_ge(prep, 6)
            dve.tensor_tensor(mixk[:, :, :], diag16[:, :].unsqueeze(1).broadcast_to([128, HEADS, IC]),
                              mixc[:, :].unsqueeze(2).broadcast_to([128, HEADS, IC]), ALU.mult)
            wait_filled(dve, "pM")
            dve.tensor_copy(M[:, :], bank("pM")[:, 0:128]).then_inc(emptied[BANK["pM"]], 1)
            wait_emptied(dve, "pM")

            def norm_stats(k, step, G):
                g = G + LAG[step]
                ps = bank(step)
                wait_filled(dve, step, G)
                for s in range(SLOTS):
                    last = dve.bn_stats(stats[k][:, s, :], ps[0:N, 128 * s:128 * s + 128])
                last.then_inc(stats_ready[k], 1)
                dve.wait_ge(stats_ready[k], g + 1)
                dve.memset(scratch[:, :], 0.0)
                for s in range(SLOTS):
                    last = dve.bn_aggr(mv[k][:, s, :], stats[k][:, s, :])
                last.then_inc(mv_ready[k], 1)

            def norm_apply(k, step, G):
                g = G + LAG[step]
                ps = bank(step)
                dve.wait_ge(rstd_ready[k], g + 1)
                for s in range(SLOTS):
                    last = dve.tensor_scalar(xn[k][:, s, :], ps[0:N, 128 * s:128 * s + 128], mv[k][:, s, 0:1],
                                             rstd[k][:, s:s + 1], ALU.subtract, ALU.mult)
                last.then_inc(emptied[BANK[step]], 1)

            def routing(G):
                g = G + LAG["RT"]
                steps = [0]

                def link(ins):
                    steps[0] += 1
                    ins.then_inc(route, 1)
                    dve.wait_ge(route, N_ROUTE * g + steps[0])

                def wide(a):
                    return a.unsqueeze(2).broadcast_to([N, SLOTS, E])

                empty("RT", G, logit[:, :, :].rearrange("p s e -> p (s e)"), bank("RT")[0:N, 0:SLOTS * E])
                wait_emptied(dve, "RT", G)
                link(dve.tensor_reduce(top[:, 0, :], logit[:, :, :], AX_X, ALU.max))
                link(dve.tensor_tensor(shift_l[:, :, :], logit[:, :, :], wide(top[:, 0, :]), ALU.subtract))
                link(dve.scalar_tensor_tensor(out=key1[:, :, :], in0=shift_l[:, :, :], scalar=0.0, in1=rev[:, :, :],
                                              op0=ALU.is_ge, op1=ALU.mult))
                link(dve.tensor_reduce(top[:, 1, :], key1[:, :, :], AX_X, ALU.max))
                link(dve.tensor_tensor(hot1[:, :, :], key1[:, :, :], wide(top[:, 1, :]), ALU.is_equal))
                link(dve.scalar_tensor_tensor(out=rest[:, :, :], in0=hot1[:, :, :], scalar=-3e38, in1=shift_l[:, :, :],
                                              op0=ALU.mult, op1=ALU.add))
                link(dve.tensor_reduce(top[:, 2, :], rest[:, :, :], AX_X, ALU.max))
                link(dve.tensor_tensor(key1[:, :, :], rest[:, :, :], wide(top[:, 2, :]), ALU.is_equal))
                link(dve.tensor_tensor(key2[:, :, :], key1[:, :, :], rev[:, :, :], ALU.mult))
                link(dve.tensor_reduce(top[:, 3, :], key2[:, :, :], AX_X, ALU.max))
                link(dve.tensor_tensor(hot2[:, :, :], key2[:, :, :], wide(top[:, 3, :]), ALU.is_equal))
                link(dve.tensor_tensor(hot1[:, :, :], hot1[:, :, :], hot2[:, :, :], ALU.add))
                dve.wait_ge(exl_ready, g + 1)
                link(dve.tensor_reduce(top[:, 4, :], exl[:, :, :], AX_X, ALU.add))
                link(dve.tensor_tensor(key1[:, :, :], exl[:, :, :], hot1[:, :, :], ALU.mult))
                link(dve.tensor_reduce(top[:, 5, :], key1[:, :, :], AX_X, ALU.add))
                link(dve.scalar_tensor_tensor(out=top[:, 6, :], in0=top[:, 4, :], scalar=1e-20, in1=top[:, 5, :],
                                              op0=ALU.mult, op1=ALU.add))
                link(dve.reciprocal(top[:, 7, :], top[:, 6, :]))
                link(dve.tensor_tensor(combine[:, :, :], key1[:, :, :], wide(top[:, 7, :]), ALU.mult))
                assert steps[0] == N_ROUTE

            def scores_max(b):
                dve.wait_ge(dots_ready, b + 1)
                at_least(dve, exp_ready, b)
                dve.tensor_reduce(negmax[:, :].rearrange("p (a c) -> p a c", a=2),
                                  ps_dots[:, :, 0:HALF * N].rearrange("p a (c j) -> p a c j", c=HALF), AX_X, ALU.max,
                                  negate=True).then_inc(max_ready, 1)

            def invert_sums(b, s):
                dve.wait_ge(exp_ready, b + 1)
                at_least(dve, probs_ready, b - 1)
                dve.reciprocal(rinv[:, s % 2, :], sums[:, s % 2, :]).then_inc(rinv_ready, 1)

            def scale_mixed(b, s):
                dve.wait_ge(arstd_ready, b + 1)
                at_least(dve, av_ready, b - 1)
                to = aT[:, (s - 1) % 2, :, :]
                mixed = ps_mix[0:N, :, 0:128 * HALF].rearrange("p a (c g i) -> p a c g i", c=HALF, g=HEADS)
                scale = arstd[:, :, :].rearrange("p (a c) i -> p a c i", a=2)
                row = STARTS[1]
                for a in range(2):
                    dst = bass.AP(tensor=to.tensor, offset=to.offset + STARTS[HALF * a],
                                  ap=[list(to.ap[0]), [row, HALF], [N, HEADS], [1, row]])
                    dve.tensor_tensor(dst, mixed[:, a, :, :, 0:row],
                                      scale[:, a, :, 0:row].unsqueeze(2).broadcast_to([N, HALF, HEADS, row]), ALU.mult)
                dve.tensor_tensor(to[:, :, STARTS[HALF] - 1::STARTS[HALF]].rearrange("p g a -> p a g"),
                                  mixed[:, :, HALF - 1, :, row],
                                  scale[:, :, HALF - 1, row].unsqueeze(2).broadcast_to([N, 2, HEADS]), ALU.mult)\
                   .then_inc(aT_ready, 1)

            def do(step, G):
                if isinstance(step, tuple):
                    kind, s = step
                    b = SLOTS * G + s - BEHIND[kind]
                    if kind == "dots":
                        scores_max(b)
                    if kind == "inv":
                        invert_sums(b, s)
                    if kind == "scale":
                        scale_mixed(b, s)
                    if kind == "av":
                        dve.wait_ge(av_ready, b + 1)
                        dve.tensor_copy(oT[:, :, (s - 2) % SLOTS, :],
                                        ps_av[:, 0:N * HEADS // 2].rearrange("p (k n) -> p k n", n=N))\
                           .then_inc(oT_ready, 1)
                    return
                if step == "shift":
                    return
                g = G + LAG[step]
                ps = bank(step)
                if step in ("Y1", "Y3", "Y5", "Y7"):
                    empty(step, G, yT[:, :, :, int(step[1]), :], chunked(ps))
                elif step == "V1":
                    empty(step, G, v_sb[:, 1, :], ps[0:N, :])
                elif step in ("TH", "TH2"):
                    k = int(step == "TH2")
                    norm_stats(k, step, G)
                    norm_apply(k, step, G)
                elif step == "OP":
                    wait_emptied(dve, "YF", G)
                    at_least(dve, shifted, G)
                    wait_filled(dve, step, G)
                    for s in range(SLOTS):
                        last = dve.scalar_tensor_tensor(out=h2T[:, s, :], in0=ps[:, N * s:N * s + N],
                                                        scalar=bias_old[:, s:s + 1], in1=hT_old[:, s, :],
                                                        op0=ALU.add, op1=ALU.add)
                    last.then_inc(emptied[BANK[step]], 1)
                elif step == "TX":
                    wait_emptied(dve, "TX", G)
                    dve.tensor_reduce(xsum[:, :], xT[:, :, :], AX_X, ALU.add).then_inc(xsum_ready, 1)
                elif step == "BS":
                    at_least(dve, shifted, G + 1)
                    wait_filled(dve, step, G)
                    dve.tensor_scalar(bias[:, :], ps[:, 0:SLOTS], vecT[:, 11:12], None, ALU.add)\
                       .then_inc(emptied[BANK[step]], 1)
                elif step == "RT":
                    routing(G)
                elif step == "CT":
                    empty(step, G, combT[:, :], ps[0:E, 0:W])
                elif step[0] == "C":
                    e = int(step[1])
                    wait_filled(dve, step, G)
                    wait_emptied(dve, f"Z{e}", G)
                    ins = dve.tensor_tensor(act1[:, e, :], ps[:, 0:W], act1[:, e, :], ALU.mult)
                    ins.then_inc(emptied[BANK[step]], 1)
                elif step == "YF":
                    wait_filled(dve, step, G)
                    dve.scalar_tensor_tensor(out=fT[:, :, :].rearrange("p s n -> p (s n)"), in0=ps[:, 0:W],
                                             scalar=vecT[:, 9:10], in1=h2T[:, :, :].rearrange("p s n -> p (s n)"),
                                             op0=ALU.add, op1=ALU.add).then_inc(emptied[BANK[step]], 1)

            run(dve, do)

        @block.gpsimd
        def _(pool):
            pool.memset(minus_half[:, :], -0.5)
            pool.memset(ones[:, :], 1.0)
            pool.memset(eps[:, :], LN_EPS).then_inc(pool_consts, 1)
            pool.wait_ge(pool_consts, 1)

            def do(step, G):
                if isinstance(step, tuple):
                    kind, s = step
                    b = SLOTS * G + s - BEHIND[kind]
                    if kind == "inv":
                        pool.wait_ge(rinv_ready, b + 1)
                        at_least(pool, mix_ready, b - 1)
                        pool.tensor_tensor(probs[:, s % 2, :, :], ex[:, s % 2, :, :],
                                           rinv[:, s % 2, :].unsqueeze(2).broadcast_to([128, CHUNKS, N]),
                                           ALU.mult).then_inc(probs_ready, 1)
                    if kind == "mix":
                        pool.wait_ge(sq_ready, b + 1)
                        pool.tensor_tensor(sum4[:, :, :, :], sq[:, :, 0:4, :], sq[:, :, 4:8, :], ALU.add)\
                            .then_inc(tree4, 1)
                        pool.wait_ge(tree4, b + 1)
                        pool.tensor_tensor(sum2[:, :, :, :], sum4[:, :, 0:2, :], sum4[:, :, 2:4, :], ALU.add)\
                            .then_inc(tree2, 1)
                        pool.wait_ge(tree2, b + 1)
                        at_least(pool, lnvar_ready, b)
                        pool.tensor_tensor(sumsq[:, :, :], sum2[:, :, 0, :], sum2[:, :, 1, :], ALU.add)\
                            .then_inc(sumsq_ready, 1)
                    return
                if step in ("TH", "TH2"):
                    k = int(step == "TH2")
                    g = G + LAG[step]
                    pool.wait_ge(mv_ready[k], g + 1)
                    pool.tensor_tensor(vare[k][:, :], mv[k][:, :, 1], eps[0:N, :], ALU.add)\
                        .then_inc(vare_ready[k], 1)
                    pool.wait_ge(vare_ready[k], g + 1)
                    pool.tensor_tensor(rstd[k][:, :], vare[k][:, :], minus_half[0:N, :], ALU.pow)\
                        .then_inc(rstd_ready[k], 1)
                if step == "shift":
                    wait_emptied(pool, "OP", G)
                    wait_emptied(pool, "TK", G - 1)
                    wait_emptied(pool, "BS", G - 1)
                    pool.tensor_tensor(bias_old[:, :], bias[:, :], ones[:, :], ALU.mult)
                    pool.tensor_copy(hT_old[:, :, :], hT[:, :, :]).then_inc(shifted, 1)

            run(pool, do)


_INS = ['x', 'L0_tok_W', 'L0_tok_b', 'L0_attn_w_qkv', 'L0_attn_reattn_w', 'L0_attn_ln_g', 'L0_attn_ln_b',
        'L0_attn_w_out', 'L0_attn_b_out', 'L0_ffn_gate_w', 'L0_ffn_w1', 'L0_ffn_b1', 'L0_ffn_w2', 'L0_ffn_b2',
        'L0_ffn_sw1', 'L0_ffn_sb1', 'L0_ffn_sw2', 'L0_ffn_sb2']


def kernel(**inputs):
    import concourse.bacc as _bacc
    from concourse.bass_utils import run_bass_kernel_spmd as _run

    nc = _bacc.Bacc("TRN2", target_bir_lowering=False, num_devices=1)
    arrays, args = {}, []
    for name in _INS:
        a = np.ascontiguousarray(inputs[name])
        arrays[f"in_{name}"] = a
        args.append(nc.dram_tensor(f"in_{name}", a.shape, mybir.dt.from_np(a.dtype), kind="ExternalInput").ap())
    consts = {"ident": np.eye(128, dtype=np.float32),
              "rev": np.broadcast_to(np.arange(E, 0, -1, dtype=np.float32), (N, SLOTS, E)).copy()}
    for name, a in consts.items():
        arrays[f"const_{name}"] = a
        args.append(nc.dram_tensor(f"const_{name}", a.shape, F32, kind="ExternalInput").ap())
    args.append(nc.dram_tensor("out_0", (B, N, D), F32, kind="ExternalOutput").ap())
    audio_tower(nc, *args)
    r = _run(nc, [arrays], core_ids=[0])
    return r.results[0]["out_0"]
```

```python
from contextlib import ExitStack

import numpy as np

import concourse.bass as bass
from concourse import mybir

F32 = mybir.dt.float32
F32R = mybir.dt.float32r
ALU = mybir.AluOpType
ACT = mybir.ActivationFunctionType
AX_X = mybir.AxisListType.X

B, T, C = 64, 750, 32
PATCH, STRIDE = 16, 8
D = 128
N = (T - PATCH) // STRIDE + 1
HEADS, DH = 8, 64
E = 8
SLOTS = 4
NG = B // SLOTS
W = SLOTS * N
NS = 96
PAIRS = STRIDE * C
NP2 = N + 1
KT = PATCH * C // D
IC = 16
CHUNKS = 6
STARTS = [0, 15, 30, 46, 61, 76]
HALF = CHUNKS // 2
LN_EPS = 1e-5
N_ROUTE = 18

BEHIND = {"dots": 0, "max": 0, "exa": 0, "exb": 0, "inv": 0, "mix": 1, "sq": 1, "rstd": 1, "scale": 1,
          "av": 2, "ev": 2}
STEPS = [
    "Z0", ("dots", 0), ("max", 0), "Z1", "Z2", ("exa", 0), ("mix", 0), ("sq", 0), ("exb", 0), "C0", "C1", "Z3",
    ("av", 0), "C2", "H0", ("ev", 0), "Z4", ("dots", 1), ("rstd", 0), ("inv", 0), "C3", "Z5", "C4", "H1", "Z6",
    "Z7", ("scale", 0), "C5", ("max", 1), "H2", ("exa", 1), "C6", "C7", "H3", ("exb", 1), ("av", 1), "Z8", "H4",
    "XE", ("mix", 1), "XO", ("ev", 1), ("dots", 2), "V2", ("max", 2), "YF", ("sq", 1), ("inv", 1), ("exa", 2),
    ("exb", 2), ("rstd", 1), "OP", "shift", "TK", ("scale", 1), ("inv", 2), "TH2", ("av", 2), "TH", ("ev", 2),
    "NH2", "NH", ("mix", 2), ("sq", 2), ("dots", 3), "TX2", ("max", 3), "V3", "TX", ("rstd", 2), "RT", "OT",
    ("scale", 2), "Y0", "Y1", "XS", "Y2", "Y3", ("mix", 3), ("exa", 3), "R2", ("exb", 3), "Y4", "BS", "Y5",
    ("sq", 3), "R3", ("av", 3), "V0", "Y6", "Y7", ("rstd", 3), "V1", ("inv", 3), ("scale", 3), "CT", ("ev", 3),
]
LAG = {"XE": 1, "XO": 1, "TK": 1, "TH": 1, "NH": 1, "TX": 1, "BS": 1, "V0": 1, "V1": 1, "V2": 0, "V3": 0,
       "OP": -1, "TH2": -1, "NH2": -1, "TX2": -1, "RT": -1, "R2": -1, "R3": -1, "CT": -1, "YF": -2, "OT": -2, "shift": 0}
LAG.update({f"Y{h}": 1 for h in range(HEADS)})
LAG.update({f"Z{e}": -2 for e in range(E + 1)})
LAG.update({f"C{e}": -2 for e in range(E)})
LAG.update({f"H{k}": -2 for k in range(E // 2 + 1)})
LAG["XS"] = 1
NO_FILL = ("shift", "NH", "NH2", "R2", "R3", "XS", "H0", "H1", "H2", "H3", "H4")
FILLS = [step for step in STEPS if isinstance(step, str) and step not in NO_FILL]
PROLOGUE = ["pT", "pO", "pV", "pA0", "pA1", "pB", "pM"]
NBANK = 3
BANK = {step: n % NBANK for n, step in enumerate(FILLS)}
BANK.update({step: n % NBANK for n, step in enumerate(PROLOGUE)})
FIRST, STEADY, END = -1, 2, NG - 2
LAST = NG + 2


def exists(n, count):
    return not isinstance(n, int) or 0 <= n < count


def present(step, G):
    if isinstance(step, tuple):
        kind, s = step
        return exists(SLOTS * G + s - BEHIND[kind], B)
    return exists(G + LAG[step], NG)


def fills_before(step, G, more=0):
    if step in PROLOGUE:
        return more + sum(BANK[p] == BANK[step] for p in PROLOGUE[:PROLOGUE.index(step)])
    total = more + sum(BANK[p] == BANK[step] for p in PROLOGUE)
    same = [other for other in FILLS if BANK[other] == BANK[step]]
    ahead = [LAG[other] + (FILLS.index(other) < FILLS.index(step)) for other in same]
    if isinstance(G, int):
        return total + sum(max(0, min(NG, G + n)) for n in ahead)
    return G * len(same) + (total + sum(ahead))


def audio_tower(nc, x, tok_W, tok_b, w_qkv, reattn_w, ln_g, ln_b, w_out, b_out, gate_w, w1, b1, w2, b2,
                sw1, sb1, sw2, sb2, ident_dram, rev_dram, out):
    with ExitStack() as ctx:
        def sb(name, shape, dt=F32):
            return ctx.enter_context(nc.sbuf_tensor(name, shape, dt))

        def split(name, shape):
            return sb(name + "_hi", shape, F32R), sb(name + "_lo", shape, F32R)

        def sem(name):
            return ctx.enter_context(nc.semaphore(name))

        ps_dots = ctx.enter_context(nc.psum_tensor("ps_dots", [128, 2, 512], F32))
        ps_mix = ctx.enter_context(nc.psum_tensor("ps_mix", [128, 2, 512], F32))
        ps_av = ctx.enter_context(nc.psum_tensor("ps_av", [128, 512], F32))
        ps_fill = [ctx.enter_context(nc.psum_tensor(f"ps_fill{k}", [128, 512], F32)) for k in range(NBANK)]

        ident = sb("ident", [128, 128])
        rev = sb("rev", [N, SLOTS, E])
        eps = sb("eps", [128, SLOTS])
        ones = sb("ones", [128, SLOTS])
        scratch = sb("scratch", [N, 1])
        minus_half = sb("minus_half", [128, SLOTS])
        qkv = sb("qkv", [128, 12, 128])
        vecs = sb("vecs", [12, 128])
        gate_nat = sb("gate_nat", [E, 128])
        b2_sb = sb("b2_sb", [E, 128])
        lng = sb("lng", [128, HEADS])
        lnb = sb("lnb", [128, HEADS])
        mixw = sb("mixw", [128, HEADS])
        mixmean = sb("mixmean", [128, 2])
        mixc = sb("mixc", [128, HEADS])
        diag16 = sb("diag16", [128, IC])
        mixk = sb("mixk", [128, HEADS, IC])
        tokT = split("tokT", [128, KT, 128])
        woT = sb("woT", [128, 4, 128])
        woT_split = split("woT_split", [128, 4, 128])
        wvT = split("wvT", [128, 4, 128])
        A = split("A", [128, HEADS, 128])
        M = sb("M", [128, 128])
        vecT = sb("vecT", [128, 32])
        w2_split = split("w2_split", [128, E + 1, 128])
        w1_split = split("w1_split", [128, E + 1, 128])
        gateT = split("gateT", [128, E])
        full = sb("full", [128, 512])
        pick = sb("pick", [64, E, 128], F32R)
        b2_both = sb("b2_both", [64, 128], F32R)
        b2_low = sb("b2_low", [E, 128], F32R)

        xin = sb("xin", [NS, SLOTS, PAIRS])
        xe = split("xe", [128, SLOTS, NP2])
        xo = split("xo", [128, SLOTS, NP2])
        hT = sb("hT", [128, SLOTS, N])
        hT_old = sb("hT_old", [128, SLOTS, N])
        stats = [sb(f"stats{k}", [N, SLOTS, 6]) for k in range(2)]
        mv = [sb(f"mv{k}", [N, SLOTS, 2]) for k in range(2)]
        vare = [sb(f"vare{k}", [N, SLOTS]) for k in range(2)]
        rstd = [sb(f"rstd{k}", [N, SLOTS]) for k in range(2)]
        xn = [sb(f"xn{k}", [NS, SLOTS, 128]) for k in range(2)]
        xT = sb("xT", [128, W + NS - N])
        xT_split = split("xT_split", [128, W])
        xsum = sb("xsum", [128, SLOTS])
        bias = sb("bias", [128, SLOTS])
        bias_old = sb("bias_old", [128, SLOTS])
        yT = sb("yT", [128, 2 * SLOTS, HALF, HEADS, IC])
        v_sb = sb("v_sb", [N, SLOTS, HEADS * DH])

        negmax = sb("negmax", [128, CHUNKS])
        sums = sb("sums", [128, 2, CHUNKS])
        rinv = sb("rinv", [128, 2, CHUNKS])
        ex = sb("ex", [128, 2, CHUNKS, N])
        probs = sb("probs", [128, 2, CHUNKS, N])
        sq = sb("sq", [N, CHUNKS, HEADS, IC])
        sum4 = sb("sum4", [N, CHUNKS, 4, IC])
        sum2 = sb("sum2", [N, CHUNKS, 2, IC])
        sumsq = sb("sumsq", [N, CHUNKS, IC])
        lnvar = sb("lnvar", [N, CHUNKS, IC])
        arstd = sb("arstd", [N, CHUNKS, IC])
        aT = sb("aT", [N, 2, HEADS * N + NS - N])
        oT = split("oT", [128, HEADS // 2, SLOTS, N])

        h2T = sb("h2T", [128, SLOTS, N])
        x2T = split("x2T", [128, W])
        logit = sb("logit", [N, SLOTS, E])
        shift_l = sb("shift_l", [N, SLOTS, E])
        exl = sb("exl", [N, SLOTS, E])
        key1 = sb("key1", [N, SLOTS, E])
        hot1 = sb("hot1", [N, SLOTS, E])
        rest = sb("rest", [N, SLOTS, E])
        key2 = sb("key2", [N, SLOTS, E])
        hot2 = sb("hot2", [N, SLOTS, E])
        top = sb("top", [N, 8, SLOTS])
        combine = sb("combine", [NS, SLOTS, E])
        combT = sb("combT", [64, W], F32R)
        act1 = sb("act1", [128, E + 1, W])
        act1_split = split("act1_split", [128, E + 1, W])

        def blocks(buffer, first, count):
            flat = buffer.rearrange("p e w -> p (e w)")
            return flat[:, 128 * first:128 * (first + count)].rearrange("p (k m) -> p k m", m=128)

        ex_rows, probs_rows = [m[:, :, :, :].rearrange("p a c n -> p a (c n)") for m in (ex, probs)]
        w1_sb = blocks(act1[:, :, :], 0, E + 1)
        w2_sb = blocks(act1[:, :, :], E + 1, E + 1)
        tok_nat = blocks(ex_rows, 0, KT)
        wo_nat = blocks(ex_rows, KT, 4)
        wv_g = blocks(probs_rows, 0, 4)
        woTb = blocks(probs_rows, 4, 4)
        fT = sb("fT", [128, SLOTS, N])
        ostage = sb("ostage", [N, SLOTS, 128])

        filled = [sem(f"filled{k}") for k in range(NBANK)]
        emptied = [sem(f"emptied{k}") for k in range(NBANK)]
        consts_loaded = sem("consts_loaded")
        experts_loaded = sem("experts_loaded")
        pool_consts = sem("pool_consts")
        x_loaded = sem("x_loaded")
        stored = sem("stored")
        halved = sem("halved")
        experts_ready = sem("experts_ready")
        prep = sem("prep")
        dots_ready = sem("dots_ready")
        max_ready = sem("max_ready")
        exp_ready = sem("exp_ready")
        rinv_ready = sem("rinv_ready")
        probs_ready = sem("probs_ready")
        oT_high = sem("oT_high")
        mix_ready = sem("mix_ready")
        sq_ready = sem("sq_ready")
        tree4 = sem("tree4")
        tree2 = sem("tree2")
        sumsq_ready = sem("sumsq_ready")
        lnvar_ready = sem("lnvar_ready")
        arstd_ready = sem("arstd_ready")
        aT_ready = sem("aT_ready")
        av_ready = sem("av_ready")
        oT_ready = sem("oT_ready")
        stats_ready = [sem(f"stats_ready{k}") for k in range(2)]
        mv_ready = [sem(f"mv_ready{k}") for k in range(2)]
        vare_ready = [sem(f"vare_ready{k}") for k in range(2)]
        rstd_ready = [sem(f"rstd_ready{k}") for k in range(2)]
        xsum_ready = sem("xsum_ready")
        high_ready = [sem(f"high_ready{k}") for k in range(3)]
        patch_high = sem("patch_high")
        xT_ready = sem("xT_ready")
        units_high = sem("units_high")
        units_ready = sem("units_ready")
        shifted = sem("shifted")
        exl_ready = sem("exl_ready")
        route = sem("route")

        def products(out, stationary, moving, start=True, stop=True):
            (s_hi, s_lo), (m_hi, m_lo) = stationary, moving
            nc.tensor.matmul(out, s_hi, m_hi, start=start, stop=False)
            nc.tensor.matmul(out, s_hi, m_lo, start=False, stop=False)
            return nc.tensor.matmul(out, s_lo, m_hi, start=False, stop=stop)

        def at_least(eng, s, value):
            if isinstance(value, int) and value <= 0:
                return
            eng.wait_ge(s, value)

        def wait_filled(eng, step, G=0):
            at_least(eng, filled[BANK[step]], fills_before(step, G, 1))

        def wait_emptied(eng, step, G=0):
            if step in PROLOGUE or present(step, G):
                at_least(eng, emptied[BANK[step]], fills_before(step, G, 1))

        def wait_free(eng, step, G=0):
            at_least(eng, emptied[BANK[step]], fills_before(step, G))

        def wait_read(eng, G, earlier, step=None):
            last = {BANK[step]: (0, FILLS.index(step), step)} if step else {}
            for other, back in earlier:
                if present(other, G - back):
                    place = (-back, FILLS.index(other), other)
                    last[BANK[other]] = max(last.get(BANK[other], place), place)
            for back, _, other in last.values():
                if other == step:
                    wait_free(eng, step, G)
                else:
                    wait_emptied(eng, other, G + back)

        def chunked(ps):
            whole = ps[:, 0:W]
            return bass.AP(tensor=whole.tensor, offset=whole.offset,
                           ap=[list(whole.ap[0]), [STARTS[HALF], 2 * SLOTS], [STARTS[1], HALF], [1, IC]])

        def patches(ps):
            return ps[:, 0:SLOTS * NS].rearrange("p (s n) -> p s n", n=NS)[:, :, 0:NP2]

        def values():
            return ps_av[:, 0:NS * HEADS // 2].rearrange("p (k n) -> p k n", n=NS)[:, :, 0:N]

        def bank(step):
            return ps_fill[BANK[step]]

        def run(eng, do):
            def iteration(G):
                for step in STEPS:
                    if present(step, G):
                        do(step, G)

            for G in range(FIRST, STEADY):
                iteration(G)
            with eng.Fori(STEADY, END) as G:
                iteration(G)
            for G in range(END, LAST):
                iteration(G)

        x_rows = x.rearrange("b t c -> b (t c)")
        x_pairs = x_rows[:, 0:NP2 * PAIRS].rearrange("b (p k) -> p b k", p=NP2)
        out_rows = out.rearrange("b p d -> p b d")

        N_CONSTS = 22

        block = ctx.enter_context(nc.Block())

        @block.sync
        def _(sp):
            def load(g):
                sp.dma_start(xin[0:NP2, :, :], x_pairs[:, bass.ds(SLOTS * g, SLOTS), :]).then_inc(x_loaded, 16)

            consts = [
                (ident[:, :], ident_dram),
                (tok_nat[:, :, :], tok_W.rearrange("d (k f) -> d k f", k=KT)),
                (vecs[0:8, :], b1), (vecs[8:9, :], sb1.unsqueeze(0)), (vecs[9:10, :], sb2.unsqueeze(0)),
                (vecs[10:11, :], tok_b.unsqueeze(0)), (vecs[11:12, :], b_out.unsqueeze(0)),
                (qkv[:, :, :], w_qkv.rearrange("(c p) d -> p c d", p=128)),
                (wo_nat[:, :, :], w_out.rearrange("d (k f) -> d k f", k=4)),
                (gate_nat[:, :], gate_w), (b2_sb[:, :], b2),
                (rev[:, :, :], rev_dram),
            ]
            for dst, src in ((lng, ln_g), (lnb, ln_b)):
                consts.append((dst[:, :], bass.AP(tensor=src.tensor, offset=0, ap=[[0, 128], [1, HEADS]])))
            for h in range(HEADS):
                consts.append((mixw[IC * h:IC * h + IC, :],
                               bass.AP(tensor=reattn_w.tensor, offset=HEADS * h, ap=[[0, IC], [1, HEADS]])))
            assert len(consts) == N_CONSTS
            sp.wait_ge(pool_consts, 1)
            load(0)
            for dst, src in consts:
                sp.dma_start(dst, src).then_inc(consts_loaded, 16)
            sp.dma_start(w1_sb[:, 0:E, :], w1.rearrange("e h f -> h e f")).then_inc(experts_loaded, 16)
            sp.dma_start(w1_sb[:, E, :], sw1).then_inc(experts_loaded, 16)
            sp.dma_start(w2_sb[:, 0:E, :], w2.rearrange("e f h -> f e h")).then_inc(experts_loaded, 16)
            sp.dma_start(w2_sb[:, E, :], sw2).then_inc(experts_loaded, 16)

            def do(step, G):
                if step == "XO" and exists(G + 2, NG):
                    wait_filled(sp, "XO", G)
                    load(G + 2)
                if step == "OT":
                    wait_emptied(sp, "OT", G)
                    sp.dma_start(out_rows[:, bass.ds(SLOTS * (G - 2), SLOTS), :],
                                 ostage[:, :, :]).then_inc(stored, 16)

            run(sp, do)
            sp.wait_ge(stored, 16 * NG)

        @block.tensor
        def _(pe):
            def fill(step, G=0):
                wait_free(pe, step, G)
                return bank(step)

            def transposes(step, G, pieces):
                for o, i, d in pieces:
                    last = pe.transpose(o, i, d)
                last.then_inc(filled[BANK[step]], 1)

            pe.wait_ge(consts_loaded, 16 * N_CONSTS)
            ps = fill("pT")
            transposes("pT", 0, [(ps[:, 128 * k:128 * k + 128], tok_nat[:, k, :], ident[:, :]) for k in range(KT)])
            ps = fill("pO")
            transposes("pO", 0, [(ps[:, 128 * k:128 * k + 128], wo_nat[:, k, :], ident[:, :]) for k in range(4)])
            pe.wait_ge(prep, 1)
            ps = fill("pV")
            transposes("pV", 0, [(ps[:, 128 * k:128 * k + 128], wv_g[:, k, :], ident[:, :]) for k in range(4)])
            for half in range(2):
                step = f"pA{half}"
                ps = fill(step)
                rows = slice(DH * half, DH * half + DH)
                for k in range(4):
                    last = pe.matmul(ps[:, 128 * k:128 * k + 128], qkv[rows, k, :], qkv[rows, 4 + k, :],
                                     start=True, stop=True)
                last.then_inc(filled[BANK[step]], 1)
            ps = fill("pB")
            transposes("pB", 0, [(ps[:, 0:12], vecs[:, :], ident[0:12, 0:12]),
                                 (ps[:, 16:24], gate_nat[:, :], ident[0:E, 0:E])])
            ps = fill("pM")
            pe.wait_ge(prep, 2)
            for k in range(4):
                last = pe.matmul(ps[:, 0:128], qkv[:, 8 + k, :], woTb[:, k, :], start=(k == 0), stop=(k == 3))
            last.then_inc(filled[BANK["pM"]], 1)
            wait_emptied(pe, "pM")

            def attention(kind, b, s):
                if kind == "dots":
                    g = G_of[0]
                    wait_read(pe, g, [("Y6", 1), ("Y7", 1)])
                    pe.wait_ge(xT_ready, g + 1)
                    at_least(pe, exp_ready, b)
                    for c in range(CHUNKS):
                        o = NS * (c % HALF)
                        last = pe.matmul(ps_dots[:, c // HALF, o:o + NS],
                                         yT[:, 2 * s + c // HALF, c % HALF, :, :].rearrange("p h i -> p (h i)"),
                                         xT[:, N * s:N * s + NS], start=True, stop=True)
                    last.then_inc(dots_ready, 1)
                elif kind == "mix":
                    pe.wait_ge(probs_ready, b + 1)
                    at_least(pe, aT_ready, b)
                    for c in range(CHUNKS):
                        o = 128 * (c % HALF)
                        last = pe.matmul(ps_mix[0:N, c // HALF, o:o + 128], probs[:, (s - 1) % 2, c, :],
                                         mixk[:, :, :].rearrange("p g i -> p (g i)"), start=True, stop=True)
                    last.then_inc(mix_ready, 1)
                else:
                    pe.wait_ge(aT_ready, b + 1)
                    at_least(pe, oT_ready, b)
                    for g in range(HEADS):
                        o = DH * (g % 2)
                        last = pe.matmul(ps_av[o:o + DH, NS * (g // 2):NS * (g // 2) + NS],
                                         v_sb[:, (s - 2) % SLOTS, DH * g:DH * g + DH], aT[:, s % 2, N * g:N * g + NS],
                                         start=True, stop=True)
                    last.then_inc(av_ready, 1)

            G_of = [0]

            def do(step, G):
                if isinstance(step, tuple):
                    kind, s = step
                    G_of[0] = G
                    if kind == "av":
                        vs = (s - 2) % SLOTS
                        wait_emptied(pe, f"V{vs}", G - 1)
                    if kind in ("dots", "mix", "av"):
                        attention(kind, SLOTS * G + s - BEHIND[kind], s)
                    return
                if step in NO_FILL:
                    return
                g = G + LAG[step]
                if step == "XE":
                    pe.wait_ge(x_loaded, 16 * g + 16)
                if step == "BS":
                    pe.wait_ge(xsum_ready, g + 1)
                if step == "OP":
                    pe.wait_ge(oT_ready, SLOTS * g + SLOTS)
                if step == "CT":
                    pe.wait_ge(route, N_ROUTE * (g + 1))
                if step == "YF":
                    pe.wait_ge(units_ready, (E // 2 + 1) * (g + 1))
                if step == "RT" and isinstance(G, int):
                    pe.wait_ge(experts_loaded, 64)
                    pe.wait_ge(experts_ready, 1)
                operands = {
                    "TK": [("XE", 0), ("XO", 0)],
                    "TH": [("TK", 0)],
                    "TH2": [("OP", 0)],
                    "TX": [("TH", 0)],
                    "TX2": [("TH2", 0)],
                    "Y0": [("TX", 0)],
                    "V0": [("TX", 0)],
                    "RT": [("TX2", 0)],
                    "Z0": [("TX2", 1)],
                    "C0": [("CT", 1)],
                    "OT": [("YF", 0)],
                }
                wait_read(pe, G, operands.get(step, []), step)
                ps = bank(step)
                done = filled[BANK[step]]
                if step in ("XE", "XO"):
                    odd = 128 * (step == "XO")
                    transposes(step, G, [(ps[:, NS * s:NS * s + NS], xin[:, s, odd:odd + 128],
                                          ident[0:NS, 0:NS]) for s in range(SLOTS)])
                elif step == "TK":
                    for k in range(KT):
                        rows = [m[:, :, k // 2:k // 2 + N] for m in (xe, xo)[k % 2]]
                        last = products(ps[:, 0:W], [w[:, k, :] for w in tokT], rows, k == 0, k == KT - 1)
                    last.then_inc(done, 1)
                elif step in ("TH", "TH2"):
                    src = hT if step == "TH" else h2T
                    transposes(step, G, [(ps[0:N, 128 * s:128 * s + 128], src[:, s, :], ident[:, :])
                                         for s in range(SLOTS)])
                elif step in ("TX", "TX2"):
                    src = xn[step == "TX2"]
                    transposes(step, G, [(ps[:, N * s:N * s + NS], src[:, s, :], ident[0:NS, 0:NS])
                                         for s in range(SLOTS)])
                elif step[0] == "Y" and step != "YF":
                    products(ps[:, 0:W], [a[:, int(step[1]), :] for a in A], [m[:, 0:W] for m in xT_split])\
                        .then_inc(done, 1)
                elif step[0] == "V":
                    o = N * int(step[1])
                    products(ps[0:N, :], [m[:, o:o + N] for m in xT_split], [w[:, :, :] for w in wvT])\
                        .then_inc(done, 1)
                elif step == "BS":
                    pe.matmul(ps[:, 0:SLOTS], M[:, :], xsum[:, :], start=True, stop=True).then_inc(done, 1)
                elif step == "OP":
                    for k in range(4):
                        last = products(ps[:, 0:W], [w[:, k, :] for w in woT_split], [m[:, k, :, :] for m in oT],
                                        k == 0, k == 3)
                    last.then_inc(done, 1)
                elif step == "RT":
                    for s in range(SLOTS):
                        last = products(ps[0:N, E * s:E * s + E], [m[:, N * s:N * s + N] for m in x2T],
                                        [w[:, :] for w in gateT])
                    last.then_inc(done, 1)
                elif step == "CT":
                    transposes(step, G, [(ps[0:E, N * s:N * s + NS], combine[:, s, :], ident[0:NS, 0:NS])
                                         for s in range(SLOTS)])
                elif step[0] == "Z":
                    products(ps[:, 0:W], [w[:, int(step[1]), :] for w in w1_split], [m[:, :] for m in x2T])\
                        .then_inc(done, 1)
                elif step[0] == "C":
                    pe.matmul(ps[:, 0:W], pick[:, int(step[1]), :], combT[:, :], start=True, stop=True)\
                      .then_inc(done, 1)
                elif step == "YF":
                    pe.matmul(ps[:, 0:W], b2_both[:, :], combT[:, :], start=True, stop=False)
                    pe.matmul(ps[:, 0:W], b2_low[:, :], combT[0:E, :], start=False, stop=False)
                    for e in range(E + 1):
                        last = products(ps[:, 0:W], [w[:, e, :] for w in w2_split],
                                        [m[:, e, :] for m in act1_split], False, e == E)
                    last.then_inc(done, 1)
                elif step == "OT":
                    transposes(step, G, [(ps[0:N, 128 * s:128 * s + 128], fT[:, s, :], ident[:, :])
                                         for s in range(SLOTS)])

            run(pe, do)

        @block.scalar
        def _(act):
            def empty(step, G, dst, src, **kw):
                wait_filled(act, step, G)
                act.activation(dst, src, kw.pop("func", ACT.Copy), **kw).then_inc(emptied[BANK[step]], 1)

            def softmax_exp(b, s, half):
                if half == 0:
                    act.wait_ge(max_ready, b + 1)
                    at_least(act, probs_ready, b - 1)
                for c in range(HALF * half, HALF * half + HALF):
                    last = act.activation(ex[:, s % 2, c, :], ps_dots[:, c // HALF, NS * (c % HALF):NS * (c % HALF) + N],
                                          ACT.Exp, bias=negmax[:, c:c + 1], accum_out=sums[:, s % 2, c:c + 1])
                if half == 1:
                    last.then_inc(exp_ready, 1)

            def square(b):
                act.wait_ge(mix_ready, b + 1)
                at_least(act, sumsq_ready, b)
                act.activation(sq[:, :, :, :].rearrange("p (a c) g i -> p a (c g i)", a=2),
                               ps_mix[0:N, :, 0:128 * HALF], ACT.Square).then_inc(sq_ready, 1)

            def attention_rstd(b):
                act.wait_ge(sumsq_ready, b + 1)
                act.activation(lnvar[:, :, :], sumsq[:, :, :], ACT.Ln, bias=eps[0:N, 0:1], scale=1.0 / HEADS)\
                   .then_inc(lnvar_ready, 1)
                at_least(act, aT_ready, b)
                act.wait_ge(lnvar_ready, b + 1)
                act.activation(arstd[:, :, :], lnvar[:, :, :], ACT.Exp, scale=-0.5).then_inc(arstd_ready, 1)

            act.preload_act_table_set("natural_log_exp_and_others")
            act.wait_ge(pool_consts, 1)
            wait_emptied(act, "pM")

            def do(step, G):
                if isinstance(step, tuple):
                    kind, s = step
                    b = SLOTS * G + s - BEHIND[kind]
                    if kind in ("exa", "exb"):
                        softmax_exp(b, s, int(kind == "exb"))
                    if kind == "ev":
                        act.wait_ge(av_ready, b + 1)
                        act.activation(oT[0][:, :, (s - 2) % SLOTS, :], values(), ACT.Copy).then_inc(oT_high, 1)
                    if kind == "sq":
                        square(b)
                    if kind == "rstd":
                        attention_rstd(b)
                    return
                g = G + LAG[step]
                if step == "R2":
                    act.wait_ge(route, N_ROUTE * g + 2)
                    act.activation(exl[:, :, :], shift_l[:, :, :], ACT.Exp).then_inc(exl_ready, 1)
                if step[0] == "H":
                    k = int(step[1])
                    last = f"C{2 * k + 1}" if k < E // 2 else f"Z{E}"
                    wait_emptied(act, last, G)
                    two = slice(2 * k, min(2 * k + 2, E + 1))
                    act.activation(act1_split[0][:, two, :], act1[:, two, :], ACT.Copy).then_inc(units_high, 1)
                if step in NO_FILL:
                    return
                ps = bank(step)
                if step in ("XE", "XO"):
                    wait_filled(act, step, G)
                    act.activation((xe if step == "XE" else xo)[0][:, :, :], patches(ps), ACT.Copy)\
                       .then_inc(patch_high, 1)
                elif step == "TK":
                    at_least(act, shifted, G + 1)
                    empty(step, G, hT[:, :, :].rearrange("p s n -> p (s n)"), ps[:, 0:W], func=ACT.Identity,
                          bias=vecT[:, 10:11])
                elif step == "TX":
                    wait_filled(act, step, G)
                    act.activation(xT_split[0][:, :], ps[:, 0:W], ACT.Copy).then_inc(high_ready[0], 1)
                elif step == "TX2":
                    wait_filled(act, step, G)
                    act.activation(x2T[0][:, :], ps[:, 0:W], ACT.Copy).then_inc(high_ready[1], 1)
                elif step == "CT":
                    wait_filled(act, step, G)
                    act.activation(combT[0:E, :], ps[0:E, 0:W], ACT.Copy).then_inc(high_ready[2], 1)
                elif step in ("Y0", "Y2", "Y4", "Y6"):
                    empty(step, G, yT[:, :, :, int(step[1]), :], chunked(ps))
                elif step in ("V0", "V2", "V3"):
                    empty(step, G, v_sb[:, int(step[1]), :], ps[0:N, :])
                elif step[0] == "Z":
                    e = int(step[1])
                    if e == 0:
                        at_least(act, units_ready, (E // 2 + 1) * g)
                        if present("YF", G - 1):
                            wait_filled(act, "YF", G - 1)
                    wait_filled(act, step, G)
                    ins = act.activation(act1[:, e, :], ps[:, 0:W], ACT.Relu, bias=vecT[:, e:e + 1])
                    ins.then_inc(emptied[BANK[step]], 1)
                elif step == "OT":
                    at_least(act, stored, 16 * g)
                    empty(step, G, ostage[:, :, :].rearrange("p s n -> p (s n)"), ps[0:N, :])

            run(act, do)

        @block.vector
        def _(dve):
            def empty(step, G, dst, src):
                wait_filled(dve, step, G)
                dve.tensor_copy(dst, src).then_inc(emptied[BANK[step]], 1)

            dve.wait_ge(consts_loaded, 16 * N_CONSTS)
            for half in range(2):
                rows = slice(DH * half, DH * half + DH)
                last = dve.tensor_tensor(wv_g[rows, :, :], qkv[rows, 8:12, :],
                                         lng[rows, half::2].unsqueeze(2).broadcast_to([DH, 4, 128]), ALU.mult)
            last.then_inc(prep, 1)
            steps = [0]

            def halves(hi, lo, value):
                dve.tensor_copy(hi, value).then_inc(halved, 1)
                steps[0] += 1
                dve.wait_ge(halved, steps[0])
                return dve.tensor_tensor(lo, value, hi.bitcast(F32), ALU.subtract)

            def by4(ap):
                return ap.rearrange("p (k m) -> p k m", k=4)

            wait_filled(dve, "pT")
            halves(tokT[0][:, :, :], tokT[1][:, :, :], by4(bank("pT")[:, :])).then_inc(emptied[BANK["pT"]], 1)
            empty("pO", 0, woT[:, :, :].rearrange("p k m -> p (k m)"), bank("pO")[:, :])
            wait_emptied(dve, "pO")
            for half in range(2):
                rows = slice(DH * half, DH * half + DH)
                last = dve.tensor_tensor(woTb[rows, :, :], woT[rows, :, :],
                                         lnb[rows, half::2].unsqueeze(2).broadcast_to([DH, 4, 128]), ALU.mult)
            last.then_inc(prep, 1)
            halves(woT_split[0][:, :, :], woT_split[1][:, :, :], woT[:, :, :])
            wait_filled(dve, "pV")
            halves(wvT[0][:, :, :], wvT[1][:, :, :], by4(bank("pV")[:, :]))\
                .then_inc(emptied[BANK["pV"]], 1)
            for half in range(2):
                step = f"pA{half}"
                wait_filled(dve, step)
                dve.tensor_scalar(full[:, :], bank(step)[:, :], float(DH) ** -0.5, None, ALU.mult)\
                   .then_inc(emptied[BANK[step]], 1)
                wait_emptied(dve, step)
                halves(A[0][:, half::2, :], A[1][:, half::2, :], by4(full[:, :]))\
                    .then_inc(halved, 1)
                steps[0] += 1
                dve.wait_ge(halved, steps[0])
            wait_filled(dve, "pB")
            dve.tensor_copy(vecT[:, 0:12], bank("pB")[:, 0:12])
            halves(gateT[0][:, :], gateT[1][:, :], bank("pB")[:, 16:24]).then_inc(emptied[BANK["pB"]], 1)
            halves(b2_both[0:E, :], b2_low[:, :], b2_sb[:, :]).then_inc(halved, 1)
            steps[0] += 1
            dve.wait_ge(pool_consts, 1)
            dve.tensor_copy(b2_both[32:32 + E, :], b2_sb[:, :])
            dve.tensor_tensor(pick[:, :, :], ident[0:64, 0:E].unsqueeze(2).broadcast_to([64, E, 128]),
                              ident[0:64, 32:32 + E].unsqueeze(2).broadcast_to([64, E, 128]), ALU.add)
            dve.tensor_reduce(mixmean[:, 0:1], mixw[:, :], AX_X, ALU.add).then_inc(prep, 1)
            dve.tensor_reduce(diag16[:, :], ident[:, :].rearrange("p (h i) -> p i h", i=IC), AX_X, ALU.add)\
               .then_inc(prep, 1)
            dve.wait_ge(prep, 4)
            dve.tensor_scalar(mixmean[:, 1:2], mixmean[:, 0:1], 1.0 / HEADS, None, ALU.mult).then_inc(prep, 1)
            dve.wait_ge(prep, 5)
            dve.tensor_scalar(mixc[:, :], mixw[:, :], mixmean[:, 1:2], None, ALU.subtract).then_inc(prep, 1)
            dve.wait_ge(prep, 6)
            dve.tensor_tensor(mixk[:, :, :], diag16[:, :].unsqueeze(1).broadcast_to([128, HEADS, IC]),
                              mixc[:, :].unsqueeze(2).broadcast_to([128, HEADS, IC]), ALU.mult)
            wait_filled(dve, "pM")
            dve.tensor_copy(M[:, :], bank("pM")[:, 0:128]).then_inc(emptied[BANK["pM"]], 1)
            wait_emptied(dve, "pM")
            dve.wait_ge(experts_loaded, 64)
            halves(w1_split[0][:, :, :], w1_split[1][:, :, :], w1_sb[:, :, :])
            halves(w2_split[0][:, :, :], w2_split[1][:, :, :], w2_sb[:, :, :]).then_inc(experts_ready, 1)

            def norm_stats(k, step, G):
                g = G + LAG[step]
                ps = bank(step)
                wait_filled(dve, step, G)
                for s in range(SLOTS):
                    last = dve.bn_stats(stats[k][:, s, :], ps[0:N, 128 * s:128 * s + 128])
                last.then_inc(stats_ready[k], 1)
                dve.wait_ge(stats_ready[k], g + 1)
                dve.memset(scratch[:, :], 0.0)
                for s in range(SLOTS):
                    last = dve.bn_aggr(mv[k][:, s, :], stats[k][:, s, :])
                last.then_inc(mv_ready[k], 1)

            def norm_apply(k, step, G):
                g = G + LAG[step]
                ps = bank(step)
                dve.wait_ge(rstd_ready[k], g + 1)
                for s in range(SLOTS):
                    last = dve.tensor_scalar(xn[k][0:N, s, :], ps[0:N, 128 * s:128 * s + 128], mv[k][:, s, 0:1],
                                             rstd[k][:, s:s + 1], ALU.subtract, ALU.mult)
                last.then_inc(emptied[BANK[step]], 1)

            def routing(step, G):
                g = G + LAG[step]
                steps = [{"RT": 0, "R2": 2, "R3": 12}[step]]

                def link(ins):
                    steps[0] += 1
                    ins.then_inc(route, 1)
                    dve.wait_ge(route, N_ROUTE * g + steps[0])

                def wide(a):
                    return a.unsqueeze(2).broadcast_to([N, SLOTS, E])

                if step == "RT":
                    empty("RT", G, logit[:, :, :].rearrange("p s e -> p (s e)"), bank("RT")[0:N, 0:SLOTS * E])
                    wait_emptied(dve, "RT", G)
                    link(dve.tensor_reduce(top[:, 0, :], logit[:, :, :], AX_X, ALU.max))
                    link(dve.tensor_tensor(shift_l[:, :, :], logit[:, :, :], wide(top[:, 0, :]), ALU.subtract))
                elif step == "R2":
                    link(dve.scalar_tensor_tensor(out=key1[:, :, :], in0=shift_l[:, :, :], scalar=0.0, in1=rev[:, :, :],
                                                  op0=ALU.is_ge, op1=ALU.mult))
                    link(dve.tensor_reduce(top[:, 1, :], key1[:, :, :], AX_X, ALU.max))
                    link(dve.tensor_tensor(hot1[:, :, :], key1[:, :, :], wide(top[:, 1, :]), ALU.is_equal))
                    link(dve.scalar_tensor_tensor(out=rest[:, :, :], in0=hot1[:, :, :], scalar=-3e38, in1=shift_l[:, :, :],
                                                  op0=ALU.mult, op1=ALU.add))
                    link(dve.tensor_reduce(top[:, 2, :], rest[:, :, :], AX_X, ALU.max))
                    link(dve.tensor_tensor(key1[:, :, :], rest[:, :, :], wide(top[:, 2, :]), ALU.is_equal))
                    link(dve.tensor_tensor(key2[:, :, :], key1[:, :, :], rev[:, :, :], ALU.mult))
                    link(dve.tensor_reduce(top[:, 3, :], key2[:, :, :], AX_X, ALU.max))
                    link(dve.tensor_tensor(hot2[:, :, :], key2[:, :, :], wide(top[:, 3, :]), ALU.is_equal))
                    link(dve.tensor_tensor(hot1[:, :, :], hot1[:, :, :], hot2[:, :, :], ALU.add))
                else:
                    dve.wait_ge(exl_ready, g + 1)
                    link(dve.tensor_reduce(top[:, 4, :], exl[:, :, :], AX_X, ALU.add))
                    link(dve.tensor_tensor(key1[:, :, :], exl[:, :, :], hot1[:, :, :], ALU.mult))
                    link(dve.tensor_reduce(top[:, 5, :], key1[:, :, :], AX_X, ALU.add))
                    link(dve.scalar_tensor_tensor(out=top[:, 6, :], in0=top[:, 4, :], scalar=1e-20, in1=top[:, 5, :],
                                                  op0=ALU.mult, op1=ALU.add))
                    link(dve.reciprocal(top[:, 7, :], top[:, 6, :]))
                    link(dve.tensor_tensor(combine[0:N, :, :], key1[:, :, :], wide(top[:, 7, :]), ALU.mult))
                assert steps[0] == {"RT": 2, "R2": 12, "R3": N_ROUTE}[step]

            def scores_max(b):
                dve.wait_ge(dots_ready, b + 1)
                at_least(dve, exp_ready, b)
                dve.tensor_reduce(negmax[:, :].rearrange("p (a c) -> p a c", a=2),
                                  ps_dots[:, :, 0:HALF * NS].rearrange("p a (c j) -> p a c j", c=HALF)[:, :, :, 0:N], AX_X, ALU.max,
                                  negate=True).then_inc(max_ready, 1)

            def invert_sums(b, s):
                dve.wait_ge(exp_ready, b + 1)
                at_least(dve, probs_ready, b - 1)
                dve.reciprocal(rinv[:, s % 2, :], sums[:, s % 2, :]).then_inc(rinv_ready, 1)

            def scale_mixed(b, s):
                dve.wait_ge(arstd_ready, b + 1)
                at_least(dve, av_ready, b - 1)
                to = aT[:, (s - 1) % 2, 0:HEADS * N].rearrange("p (g n) -> p g n", n=N)
                mixed = ps_mix[0:N, :, 0:128 * HALF].rearrange("p a (c g i) -> p a c g i", c=HALF, g=HEADS)
                scale = arstd[:, :, :].rearrange("p (a c) i -> p a c i", a=2)
                row = STARTS[1]
                for a in range(2):
                    dst = bass.AP(tensor=to.tensor, offset=to.offset + STARTS[HALF * a],
                                  ap=[list(to.ap[0]), [row, HALF], [N, HEADS], [1, row]])
                    dve.tensor_tensor(dst, mixed[:, a, :, :, 0:row],
                                      scale[:, a, :, 0:row].unsqueeze(2).broadcast_to([N, HALF, HEADS, row]), ALU.mult)
                dve.tensor_tensor(to[:, :, STARTS[HALF] - 1::STARTS[HALF]].rearrange("p g a -> p a g"),
                                  mixed[:, :, HALF - 1, :, row],
                                  scale[:, :, HALF - 1, row].unsqueeze(2).broadcast_to([N, 2, HEADS]), ALU.mult)\
                   .then_inc(aT_ready, 1)

            def do(step, G):
                if isinstance(step, tuple):
                    kind, s = step
                    b = SLOTS * G + s - BEHIND[kind]
                    if kind == "max":
                        scores_max(b)
                    if kind == "inv":
                        invert_sums(b, s)
                    if kind == "scale":
                        scale_mixed(b, s)
                    if kind == "ev":
                        dve.wait_ge(oT_high, b + 1)
                        hi, lo = [m[:, :, (s - 2) % SLOTS, :] for m in oT]
                        dve.tensor_tensor(lo, values(), hi.bitcast(F32), ALU.subtract).then_inc(oT_ready, 1)
                    return
                if step in ("RT", "R2", "R3"):
                    routing(step, G)
                if step == "XS":
                    dve.wait_ge(xT_ready, G + LAG[step] + 1)
                    dve.tensor_reduce(xsum[:, :], xT[:, 0:W].rearrange("p (s n) -> p s n", n=N), AX_X, ALU.add)\
                       .then_inc(xsum_ready, 1)
                if step in ("NH", "NH2"):
                    k = int(step == "NH2")
                    norm_apply(k, ("TH", "TH2")[k], G)
                if step in NO_FILL:
                    return
                g = G + LAG[step]
                ps = bank(step)
                if step in ("Y1", "Y3", "Y5", "Y7"):
                    empty(step, G, yT[:, :, :, int(step[1]), :], chunked(ps))
                elif step in ("XE", "XO"):
                    dve.wait_ge(patch_high, 2 * g + 1 + (step == "XO"))
                    hi, lo = [m[:, :, :] for m in (xe if step == "XE" else xo)]
                    dve.tensor_tensor(lo, patches(ps), hi.bitcast(F32), ALU.subtract)\
                       .then_inc(emptied[BANK[step]], 1)
                elif step == "V1":
                    empty(step, G, v_sb[:, 1, :], ps[0:N, :])
                elif step in ("TH", "TH2"):
                    norm_stats(int(step == "TH2"), step, G)
                elif step == "OP":
                    wait_emptied(dve, "YF", G)
                    at_least(dve, shifted, G)
                    wait_filled(dve, step, G)
                    for s in range(SLOTS):
                        last = dve.scalar_tensor_tensor(out=h2T[:, s, :], in0=ps[:, N * s:N * s + N],
                                                        scalar=bias_old[:, s:s + 1], in1=hT_old[:, s, :],
                                                        op0=ALU.add, op1=ALU.add)
                    last.then_inc(emptied[BANK[step]], 1)
                elif step in ("TX", "TX2"):
                    hi, lo = xT_split if step == "TX" else x2T
                    dve.wait_ge(high_ready[int(step == "TX2")], g + 1)
                    dve.tensor_tensor(lo[:, :], ps[:, 0:W], hi[:, :].bitcast(F32), ALU.subtract)\
                       .then_inc(emptied[BANK[step]], 1)
                elif step == "BS":
                    at_least(dve, shifted, G + 1)
                    wait_filled(dve, step, G)
                    dve.tensor_scalar(bias[:, :], ps[:, 0:SLOTS], vecT[:, 11:12], None, ALU.add)\
                       .then_inc(emptied[BANK[step]], 1)
                elif step == "CT":
                    dve.wait_ge(high_ready[2], g + 1)
                    dve.tensor_tensor(combT[32:32 + E, :], ps[0:E, 0:W], combT[0:E, :].bitcast(F32), ALU.subtract)\
                       .then_inc(emptied[BANK[step]], 1)
                elif step[0] == "C":
                    e = int(step[1])
                    wait_filled(dve, step, G)
                    wait_emptied(dve, f"Z{e}", G)
                    ins = dve.tensor_tensor(act1[:, e, :], ps[:, 0:W], act1[:, e, :], ALU.mult)
                    ins.then_inc(emptied[BANK[step]], 1)
                elif step == "YF":
                    wait_filled(dve, step, G)
                    dve.scalar_tensor_tensor(out=fT[:, :, :].rearrange("p s n -> p (s n)"), in0=ps[:, 0:W],
                                             scalar=vecT[:, 9:10], in1=h2T[:, :, :].rearrange("p s n -> p (s n)"),
                                             op0=ALU.add, op1=ALU.add).then_inc(emptied[BANK[step]], 1)

            run(dve, do)

        @block.gpsimd
        def _(pool):
            pool.memset(minus_half[:, :], -0.5)
            pool.memset(xin[:, :, :], 0.0)
            for tile in xn:
                pool.memset(tile[:, :, :], 0.0)
            pool.memset(combine[:, :, :], 0.0)
            pool.memset(combT[:, :].bitcast(F32), 0.0)
            pool.memset(b2_both[:, :].bitcast(F32), 0.0)
            pool.memset(xT[:, W:], 0.0)
            pool.memset(aT[:, :, HEADS * N:], 0.0)
            pool.memset(ones[:, :], 1.0)
            pool.memset(eps[:, :], LN_EPS).then_inc(pool_consts, 1)
            pool.wait_ge(pool_consts, 1)

            def do(step, G):
                if isinstance(step, tuple):
                    kind, s = step
                    b = SLOTS * G + s - BEHIND[kind]
                    if kind == "inv":
                        pool.wait_ge(rinv_ready, b + 1)
                        at_least(pool, mix_ready, b - 1)
                        pool.tensor_tensor(probs[:, s % 2, :, :], ex[:, s % 2, :, :],
                                           rinv[:, s % 2, :].unsqueeze(2).broadcast_to([128, CHUNKS, N]),
                                           ALU.mult).then_inc(probs_ready, 1)
                    if kind == "sq":
                        pool.wait_ge(sq_ready, b + 1)
                        pool.tensor_tensor(sum4[:, :, :, :], sq[:, :, 0:4, :], sq[:, :, 4:8, :], ALU.add)\
                            .then_inc(tree4, 1)
                        pool.wait_ge(tree4, b + 1)
                        pool.tensor_tensor(sum2[:, :, :, :], sum4[:, :, 0:2, :], sum4[:, :, 2:4, :], ALU.add)\
                            .then_inc(tree2, 1)
                        pool.wait_ge(tree2, b + 1)
                        at_least(pool, lnvar_ready, b)
                        pool.tensor_tensor(sumsq[:, :, :], sum2[:, :, 0, :], sum2[:, :, 1, :], ALU.add)\
                            .then_inc(sumsq_ready, 1)
                    return
                if step == "XS":
                    g = G + LAG[step]
                    wait_emptied(pool, "TX", G)
                    at_least(pool, xsum_ready, g)
                    hi, lo = [m[:, :].bitcast(F32) for m in xT_split]
                    pool.tensor_tensor(xT[:, 0:W], hi, lo, ALU.add).then_inc(xT_ready, 1)
                if step[0] == "H":
                    k = int(step[1])
                    pool.wait_ge(units_high, (E // 2 + 1) * (G + LAG[step]) + k + 1)
                    hi, lo = [m[:, 2 * k:min(2 * k + 2, E + 1), :] for m in act1_split]
                    pool.tensor_tensor(lo, act1[:, 2 * k:min(2 * k + 2, E + 1), :], hi.bitcast(F32), ALU.subtract)\
                        .then_inc(units_ready, 1)
                if step in ("NH", "NH2"):
                    k = int(step == "NH2")
                    g = G + LAG[step]
                    pool.wait_ge(mv_ready[k], g + 1)
                    pool.tensor_tensor(vare[k][:, :], mv[k][:, :, 1], eps[0:N, :], ALU.add)\
                        .then_inc(vare_ready[k], 1)
                    pool.wait_ge(vare_ready[k], g + 1)
                    pool.tensor_tensor(rstd[k][:, :], vare[k][:, :], minus_half[0:N, :], ALU.pow)\
                        .then_inc(rstd_ready[k], 1)
                if step == "shift":
                    wait_read(pool, G, [("OP", 0), ("TK", 1), ("BS", 1)])
                    pool.tensor_tensor(bias_old[:, :], bias[:, :], ones[:, :], ALU.mult)
                    pool.tensor_copy(hT_old[:, :, :], hT[:, :, :]).then_inc(shifted, 1)

            run(pool, do)


_INS = ['x', 'L0_tok_W', 'L0_tok_b', 'L0_attn_w_qkv', 'L0_attn_reattn_w', 'L0_attn_ln_g', 'L0_attn_ln_b',
        'L0_attn_w_out', 'L0_attn_b_out', 'L0_ffn_gate_w', 'L0_ffn_w1', 'L0_ffn_b1', 'L0_ffn_w2', 'L0_ffn_b2',
        'L0_ffn_sw1', 'L0_ffn_sb1', 'L0_ffn_sw2', 'L0_ffn_sb2']


def kernel(**inputs):
    import concourse.bacc as _bacc
    from concourse.bass_utils import run_bass_kernel_spmd as _run

    nc = _bacc.Bacc("TRN2", target_bir_lowering=False, num_devices=1)
    arrays, args = {}, []
    for name in _INS:
        a = np.ascontiguousarray(inputs[name])
        arrays[f"in_{name}"] = a
        args.append(nc.dram_tensor(f"in_{name}", a.shape, mybir.dt.from_np(a.dtype), kind="ExternalInput").ap())
    consts = {"ident": np.eye(128, dtype=np.float32),
              "rev": np.broadcast_to(np.arange(E, 0, -1, dtype=np.float32), (N, SLOTS, E)).copy()}
    for name, a in consts.items():
        arrays[f"const_{name}"] = a
        args.append(nc.dram_tensor(f"const_{name}", a.shape, F32, kind="ExternalInput").ap())
    args.append(nc.dram_tensor("out_0", (B, N, D), F32, kind="ExternalOutput").ap())
    audio_tower(nc, *args)
    r = _run(nc, [arrays], core_ids=[0])
    return r.results[0]["out_0"]
```

```python
from contextlib import ExitStack

import numpy as np

import concourse.bass as bass
from concourse import mybir

F32 = mybir.dt.float32
F32R = mybir.dt.float32r
ALU = mybir.AluOpType
ACT = mybir.ActivationFunctionType
AX_X = mybir.AxisListType.X

B, T, C = 64, 750, 32
PATCH, STRIDE = 16, 8
D = 128
N = (T - PATCH) // STRIDE + 1
HEADS, DH = 8, 64
E = 8
SLOTS = 4
NG = B // SLOTS
W = SLOTS * N
NS = 96
PAIRS = STRIDE * C
NP2 = N + 1
KT = PATCH * C // D
IC = 16
CHUNKS = 6
STARTS = [0, 15, 30, 46, 61, 76]
HALF = CHUNKS // 2
LN_EPS = 1e-5
N_ROUTE = 18

BEHIND = {"dots": 0, "max": 0, "exa": 0, "exb": 0, "inv": 0, "mix": 1, "sq": 1, "rstd": 1, "scale": 1,
          "av": 2, "ev": 2}
STEPS = [
    ("dots", 0), "Z0", ("max", 0), "Z1", "Z2", "Z3", "Z4", "C0", ("mix", 0), ("exa", 0), ("sq", 0), "C1", "C2",
    ("exb", 0), ("inv", 0), ("av", 0), ("ev", 0), "Z5", "C3", "C4", ("dots", 1), "C5", "H0", ("rstd", 0),
    ("scale", 0), "Z6", ("max", 1), "Z7", "H2", "Z8", "C6", "C7", "H1", "H4", "H3", ("av", 1), "V2", "XE",
    ("ev", 1), "XO", ("exa", 1), ("mix", 1), ("exb", 1), "YF", ("sq", 1), "OP", "shift", ("rstd", 1), ("scale", 1),
    ("inv", 1), "TK", "TH2", ("dots", 2), ("max", 2), ("exa", 2), "TH", "NH2", ("mix", 2), ("exb", 2), ("av", 2),
    ("ev", 2), "NH", ("sq", 2), "V3", "TX2", ("dots", 3), ("max", 3), "TX", ("rstd", 2), ("inv", 2), "RT", "V0",
    "Y0", ("scale", 2), "Y1", "XS", "Y2", ("exa", 3), "Y3", "R2", "Y4", "OT", ("mix", 3), "Y5", "R3", ("sq", 3),
    "Y6", "BS", ("exb", 3), ("av", 3), ("rstd", 3), "Y7", "V1", ("inv", 3), "CT", ("ev", 3), ("scale", 3),
]
LAG = {"XE": 1, "XO": 1, "TK": 1, "TH": 1, "NH": 1, "TX": 1, "BS": 1, "V0": 1, "V1": 1, "V2": 0, "V3": 0,
       "OP": -1, "TH2": -1, "NH2": -1, "TX2": -1, "RT": -1, "R2": -1, "R3": -1, "CT": -1, "YF": -2, "OT": -2,
       "shift": 0}
LAG.update({f"Y{h}": 1 for h in range(HEADS)})
LAG.update({f"Z{e}": -2 for e in range(E + 1)})
LAG.update({f"C{e}": -2 for e in range(E)})
LAG.update({f"H{k}": -2 for k in range(E // 2 + 1)})
LAG["XS"] = 1
NO_FILL = ("shift", "NH", "NH2", "R2", "R3", "XS", "H0", "H1", "H2", "H3", "H4")
FILLS = [step for step in STEPS if isinstance(step, str) and step not in NO_FILL]
UNITS_BY_POOL = ("H0", "H2", "H4")
UNITS = ("H0", "H1", "H2", "H3", "H4")
NBANK = 3
BANK = {step: n % NBANK for n, step in enumerate(FILLS)}
BANK.update({"pT": 2, "pB": 0, "pA0": 2, "pA1": 1, "pV": 2, "pO": 1, "pM": 2})
LAYOUT = ("pT", "pB", "pA0", "pA1", "prepW", "pV", "prepX", "pO", "pM", "prepE")
SETUP_START = ["XE", "XO", "pT", "pB", "TK", "pA0", "TH", "pA1", "prepW", "NH", "pV", "TX", "pO", "prepX"]
SPLIT_STEPS = ["pT", "pA0", "pA1", "pV", "pO"]
FIRST, STEADY, END = -1, 2, NG - 2
LAST = NG + 2


def exists(n, count):
    return not isinstance(n, int) or 0 <= n < count


def present(step, G):
    if isinstance(step, tuple):
        kind, s = step
        return exists(SLOTS * G + s - BEHIND[kind], B)
    return exists(G + LAG[step], NG)


ORDER_0 = [
    ("dots", 0), ("max", 0), "XE", ("exa", 0), ("exb", 0), ("inv", 0), "XO", "V2", ("dots", 1), ("max", 1),
    ("exa", 1), ("mix", 1), "shift", ("sq", 1), ("exb", 1), ("inv", 1), "TK", ("rstd", 1), "TH", ("dots", 2),
    ("max", 2), ("scale", 1), "NH", "V3", ("exa", 2), ("exb", 2), ("mix", 2), ("sq", 2), ("dots", 3), ("inv", 2),
    ("max", 3), "TX", ("av", 2), ("rstd", 2), ("scale", 2), "XS", "Y0", "Y1", "Y2", ("exa", 3), "Y3", ("mix", 3),
    ("ev", 2), ("sq", 3), "BS", "Y4", "Y5", ("av", 3), ("exb", 3), ("inv", 3), ("ev", 3), "Y6", ("rstd", 3), "Y7",
    ("scale", 3), "V0", "V1",
]
ORDERS_END = [[
    "Z0", ("dots", 0), ("max", 0), "Z1", "Z2", "Z3", ("mix", 0), "C0", ("exa", 0), ("sq", 0), "C1", "Z4", "H0",
    ("exb", 0), "Z5", "C2", "C3", ("av", 0), "C4", "Z6", "C5", ("rstd", 0), ("dots", 1), ("inv", 0), ("scale", 0),
    ("ev", 0), "H2", "Z7", "Z8", "C6", "C7", "H1", "H4", "H3", ("mix", 1), ("max", 1), "V2", ("sq", 1), ("av", 1),
    ("exa", 1), ("ev", 1), ("exb", 1), ("rstd", 1), ("scale", 1), "YF", ("inv", 1), "OP", ("dots", 2), ("max", 2),
    "TH2", ("exa", 2), "shift", "NH2", ("av", 2), ("mix", 2), ("exb", 2), ("sq", 2), ("dots", 3), ("max", 3),
    ("ev", 2), "TX2", ("rstd", 2), ("scale", 2), ("inv", 2), ("exa", 3), "RT", "R2", "R3", "OT", ("mix", 3),
    ("sq", 3), ("exb", 3), ("av", 3), "V3", ("inv", 3), ("ev", 3), "CT", ("rstd", 3), ("scale", 3),
], [
    "Z0", "Z1", "Z2", "Z3", "Z4", "C0", "C1", ("mix", 0), "C2", "H0", ("sq", 0), "Z5", "C3", "C4", "C5", "H1",
    "Z6", "H2", "Z7", ("av", 0), "C6", ("ev", 0), "Z8", ("rstd", 0), "C7", ("scale", 0), "H4", ("av", 1), "H3",
    ("ev", 1), "YF", "OP", "OT", "TH2", "NH2", "TX2", "RT", "R2", "R3", "CT",
], [
    "Z0", "Z1", "Z2", "Z3", "C0", "Z4", "C1", "Z5", "C2", "C3", "H0", "C4", "C5", "H1", "Z6", "H2", "Z7", "C6",
    "Z8", "C7", "H4", "H3", "YF", "OT",
]]


def order(G):
    if isinstance(G, int) and G == 0:
        return ORDER_0
    if isinstance(G, int) and G >= LAST - len(ORDERS_END):
        return ORDERS_END[G - LAST]
    return STEPS


SETUP = SETUP_START + [step for step in STEPS if present(step, FIRST) and step not in SETUP_START]
SETUP[SETUP.index("Y5"):SETUP.index("Y5")] = ["pM"]
SETUP += ["prepE"]

TAIL = [(step, G) for G in range(END, LAST) for step in order(G) if present(step, G)]


def fills_before(step, G, more=0):
    if step in LAYOUT or (isinstance(G, int) and G == FIRST):
        return more + sum(BANK.get(other) == BANK[step] for other in SETUP[:SETUP.index(step)])
    total = more + sum(BANK.get(other) == BANK[step] for other in LAYOUT)
    same = [other for other in FILLS if BANK[other] == BANK[step]]
    ahead = [LAG[other] + (FILLS.index(other) < FILLS.index(step)) for other in same]
    if isinstance(G, int) and G == 0:
        filled_then = [other for other in ORDER_0[:ORDER_0.index(step)] if present(other, G)] + SETUP
        return more + sum(BANK.get(other) == BANK[step] for other in filled_then)
    if isinstance(G, int) and G >= END:
        total += sum(min(NG, END + LAG[other]) for other in same)
        return total + sum(BANK.get(other) == BANK[step] for other, _ in TAIL[:TAIL.index((step, G))])
    if isinstance(G, int):
        return total + sum(max(0, min(NG, G + n)) for n in ahead)
    return G * len(same) + (total + sum(ahead))


def audio_tower(nc, x, tok_W, tok_b, w_qkv, reattn_w, ln_g, ln_b, w_out, b_out, gate_w, w1, b1, w2, b2,
                sw1, sb1, sw2, sb2, ident_dram, rev_dram, out):
    with ExitStack() as ctx:
        def sb(name, shape, dt=F32):
            return ctx.enter_context(nc.sbuf_tensor(name, shape, dt))

        def split(name, shape):
            return sb(name + "_hi", shape, F32R), sb(name + "_lo", shape, F32R)

        def sem(name):
            return ctx.enter_context(nc.semaphore(name))

        ps_dots = ctx.enter_context(nc.psum_tensor("ps_dots", [128, 2, 512], F32))
        ps_mix = ctx.enter_context(nc.psum_tensor("ps_mix", [128, 2, 512], F32))
        ps_av = ctx.enter_context(nc.psum_tensor("ps_av", [128, 512], F32))
        ps_fill = [ctx.enter_context(nc.psum_tensor(f"ps_fill{k}", [128, 512], F32)) for k in range(NBANK)]

        ident = sb("ident", [128, 128])
        rev = sb("rev", [N, SLOTS, E])
        eps = sb("eps", [128, SLOTS])
        ones = sb("ones", [128, SLOTS])
        scratch = sb("scratch", [N, 1])
        minus_half = sb("minus_half", [128, SLOTS])
        qkv = sb("qkv", [128, 12, 128])
        vecs = sb("vecs", [12, 128])
        gate_nat = sb("gate_nat", [E, 128])
        b2_sb = sb("b2_sb", [E, 128])
        lng = sb("lng", [128, HEADS])
        lnb = sb("lnb", [128, HEADS])
        mixw = sb("mixw", [128, HEADS])
        mixmean = sb("mixmean", [128, 2])
        mixc = sb("mixc", [128, HEADS])
        diag16 = sb("diag16", [128, IC])
        mixk = sb("mixk", [128, HEADS, IC])
        tokT = split("tokT", [128, KT, 128])
        woT_split = split("woT_split", [128, 4, 128])
        wvT = split("wvT", [128, 4, 128])
        A = split("A", [128, HEADS, 128])
        M = sb("M", [128, 128])
        vecT = sb("vecT", [128, 32])
        w2_split = split("w2_split", [128, E + 1, 128])
        w1_split = split("w1_split", [128, E + 1, 128])
        gateT = split("gateT", [128, E])
        pick = sb("pick", [64, E, 128], F32R)
        b2_both = sb("b2_both", [64, 128], F32R)
        b2_low = sb("b2_low", [E, 128], F32R)

        xin = sb("xin", [NS, SLOTS, PAIRS])
        xe = split("xe", [128, SLOTS, NP2])
        xo = split("xo", [128, SLOTS, NP2])
        hT = sb("hT", [128, SLOTS, N])
        hT_old = sb("hT_old", [128, SLOTS, N])
        stats = [sb(f"stats{k}", [N, SLOTS, 6]) for k in range(2)]
        mv = [sb(f"mv{k}", [N, SLOTS, 2]) for k in range(2)]
        vare = [sb(f"vare{k}", [N, SLOTS]) for k in range(2)]
        rstd = [sb(f"rstd{k}", [N, SLOTS]) for k in range(2)]
        xn = [sb(f"xn{k}", [NS, SLOTS, 128]) for k in range(2)]
        xT = sb("xT", [128, W + NS - N])
        xT_split = split("xT_split", [128, W])
        xsum = sb("xsum", [128, SLOTS])
        bias = sb("bias", [128, SLOTS])
        bias_old = sb("bias_old", [128, SLOTS])
        yT = sb("yT", [128, 2 * SLOTS, HALF, HEADS, IC])
        v_sb = sb("v_sb", [N, SLOTS, HEADS * DH])

        negmax = sb("negmax", [128, CHUNKS])
        sums = sb("sums", [128, 2, CHUNKS])
        rinv = sb("rinv", [128, 2, CHUNKS])
        ex = sb("ex", [128, 2, CHUNKS, N])
        probs = sb("probs", [128, 2, CHUNKS, N])
        sq = sb("sq", [N, CHUNKS, HEADS, IC])
        sum4 = sb("sum4", [N, CHUNKS, 4, IC])
        sum2 = sb("sum2", [N, CHUNKS, 2, IC])
        sumsq = sb("sumsq", [N, CHUNKS, IC])
        lnvar = sb("lnvar", [N, CHUNKS, IC])
        arstd = sb("arstd", [N, CHUNKS, IC])
        aT = sb("aT", [N, 2, HEADS * N + NS - N])
        oT = split("oT", [128, HEADS // 2, SLOTS, N])

        h2T = sb("h2T", [128, SLOTS, N])
        x2T = split("x2T", [128, W])
        logit = sb("logit", [N, SLOTS, E])
        shift_l = sb("shift_l", [N, SLOTS, E])
        exl = sb("exl", [N, SLOTS, E])
        key1 = sb("key1", [N, SLOTS, E])
        hot1 = sb("hot1", [N, SLOTS, E])
        rest = sb("rest", [N, SLOTS, E])
        key2 = sb("key2", [N, SLOTS, E])
        hot2 = sb("hot2", [N, SLOTS, E])
        top = sb("top", [N, 8, SLOTS])
        combine = sb("combine", [NS, SLOTS, E])
        combT = sb("combT", [64, W], F32R)
        act1 = sb("act1", [128, E + 1, W])
        act1_split = split("act1_split", [128, E + 1, W])

        def blocks(buffer, first, count):
            flat = buffer.rearrange("p e w -> p (e w)")
            return flat[:, 128 * first:128 * (first + count)].rearrange("p (k m) -> p k m", m=128)

        ex_rows, probs_rows = [m[:, :, :, :].rearrange("p a c n -> p a (c n)") for m in (ex, probs)]
        w1_sb = blocks(act1[:, :, :], 0, E + 1)
        w2_sb = blocks(act1[:, :, :], E + 1, E + 1)
        tok_nat = blocks(ex_rows, 0, KT)
        wo_nat = blocks(ex_rows, KT, 4)
        wv_g = blocks(probs_rows, 0, 4)
        woTb = blocks(probs_rows, 4, 4)
        fT = sb("fT", [128, SLOTS, N])
        ostage = sb("ostage", [N, SLOTS, 128])

        filled = [sem(f"filled{k}") for k in range(NBANK)]
        emptied = [sem(f"emptied{k}") for k in range(NBANK)]
        ident_loaded = sem("ident_loaded")
        first_loaded = sem("first_loaded")
        qkv_loaded = sem("qkv_loaded")
        consts_loaded = sem("consts_loaded")
        experts_loaded = sem("experts_loaded")
        xin_cleared = sem("xin_cleared")
        pool_consts = sem("pool_consts")
        x_loaded = sem("x_loaded")
        stored = sem("stored")
        halved = sem("halved")
        weight_high = sem("weight_high")
        wv_g_ready = sem("wv_g_ready")
        mixk_ready = sem("mixk_ready")
        experts_high = sem("experts_high")
        experts_ready = sem("experts_ready")
        prep = sem("prep")
        dots_ready = sem("dots_ready")
        max_ready = sem("max_ready")
        exp_ready = sem("exp_ready")
        rinv_ready = sem("rinv_ready")
        probs_ready = sem("probs_ready")
        oT_high = sem("oT_high")
        mix_ready = sem("mix_ready")
        sq_ready = sem("sq_ready")
        tree4 = sem("tree4")
        tree2 = sem("tree2")
        sumsq_ready = sem("sumsq_ready")
        lnvar_ready = sem("lnvar_ready")
        arstd_ready = sem("arstd_ready")
        aT_ready = sem("aT_ready")
        av_ready = sem("av_ready")
        oT_ready = sem("oT_ready")
        stats_ready = [sem(f"stats_ready{k}") for k in range(2)]
        mv_ready = [sem(f"mv_ready{k}") for k in range(2)]
        vare_ready = [sem(f"vare_ready{k}") for k in range(2)]
        rstd_ready = [sem(f"rstd_ready{k}") for k in range(2)]
        xsum_ready = sem("xsum_ready")
        high_ready = [sem(f"high_ready{k}") for k in range(3)]
        patch_high = sem("patch_high")
        xT_ready = sem("xT_ready")
        units_high = sem("units_high")
        units_ready = sem("units_ready")
        shifted = sem("shifted")
        exl_ready = sem("exl_ready")
        route = sem("route")

        def products(out, stationary, moving, start=True, stop=True):
            (s_hi, s_lo), (m_hi, m_lo) = stationary, moving
            nc.tensor.matmul(out, s_hi, m_hi, start=start, stop=False)
            nc.tensor.matmul(out, s_hi, m_lo, start=False, stop=False)
            return nc.tensor.matmul(out, s_lo, m_hi, start=False, stop=stop)

        def at_least(eng, s, value):
            if isinstance(value, int) and value <= 0:
                return
            eng.wait_ge(s, value)

        def wait_filled(eng, step, G=0):
            at_least(eng, filled[BANK[step]], fills_before(step, G, 1))

        def wait_emptied(eng, step, G=0):
            if step in LAYOUT or present(step, G):
                at_least(eng, emptied[BANK[step]], fills_before(step, G, 1))

        def wait_free(eng, step, G=0):
            at_least(eng, emptied[BANK[step]], fills_before(step, G))

        def wait_read(eng, G, earlier, step=None):
            def position(other, back):
                if isinstance(G, int):
                    return fills_before(other, G - back)
                return FILLS.index(other) - back * len(FILLS)

            last = {BANK[step]: (position(step, 0), 0, step)} if step else {}
            for other, back in earlier:
                if present(other, G - back):
                    place = (position(other, back), back, other)
                    last[BANK[other]] = max(last.get(BANK[other], place), place)
            for _, back, other in last.values():
                if other == step:
                    wait_free(eng, step, G)
                else:
                    wait_emptied(eng, other, G - back)

        def chunked(ps):
            whole = ps[:, 0:W]
            return bass.AP(tensor=whole.tensor, offset=whole.offset,
                           ap=[list(whole.ap[0]), [STARTS[HALF], 2 * SLOTS], [STARTS[1], HALF], [1, IC]])

        def patches(ps):
            return ps[:, 0:SLOTS * NS].rearrange("p (s n) -> p s n", n=NS)[:, :, 0:NP2]

        def values():
            return ps_av[:, 0:NS * HEADS // 2].rearrange("p (k n) -> p k n", n=NS)[:, :, 0:N]

        def by4(ap):
            return ap.rearrange("p (k m) -> p k m", k=4)

        def weight_parts(step):
            (hi, lo), pick_heads, scale = {
                "pT": (tokT, slice(0, 4), 1.0), "pV": (wvT, slice(0, 4), 1.0), "pO": (woT_split, slice(0, 4), 1.0),
                "pA0": (A, slice(0, HEADS, 2), DH ** -0.5), "pA1": (A, slice(1, HEADS, 2), DH ** -0.5)}[step]
            return hi[:, pick_heads, :], lo[:, pick_heads, :], scale

        def low_units(eng, step, G):
            k = int(step[1])
            two = slice(2 * k, min(2 * k + 2, E + 1))
            before = [other for other in order(G) if other in UNITS].index(step)
            eng.wait_ge(units_high, len(UNITS) * (G + LAG[step]) + before + 1)
            hi, lo = [m[:, two, :] for m in act1_split]
            eng.tensor_tensor(lo, act1[:, two, :], hi.bitcast(F32), ALU.subtract).then_inc(units_ready, 1)

        def bank(step):
            return ps_fill[BANK[step]]

        def run(eng, do, prepare=None):
            def iteration(G):
                for step in order(G):
                    if present(step, G):
                        do(step, G)

            for step in SETUP:
                if step not in LAYOUT:
                    do(step, FIRST)
                elif prepare:
                    prepare(step)
            for G in range(FIRST + 1, STEADY):
                iteration(G)
            with eng.Fori(STEADY, END) as G:
                iteration(G)
            for step, G in TAIL:
                do(step, G)

        x_rows = x.rearrange("b t c -> b (t c)")
        x_pairs = x_rows[:, 0:NP2 * PAIRS].rearrange("b (p k) -> p b k", p=NP2)
        out_rows = out.rearrange("b p d -> p b d")

        N_FIRST, N_CONSTS = 7, 13

        block = ctx.enter_context(nc.Block())

        @block.sync
        def _(sp):
            def load(g):
                sp.dma_start(xin[0:NP2, :, :], x_pairs[:, bass.ds(SLOTS * g, SLOTS), :]).then_inc(x_loaded, 16)

            first = [
                (tok_nat[:, :, :], tok_W.rearrange("d (k f) -> d k f", k=KT)),
                (vecs[0:8, :], b1), (vecs[8:9, :], sb1.unsqueeze(0)), (vecs[9:10, :], sb2.unsqueeze(0)),
                (vecs[10:11, :], tok_b.unsqueeze(0)), (vecs[11:12, :], b_out.unsqueeze(0)),
                (gate_nat[:, :], gate_w),
            ]
            consts = [
                (lng[:, :], bass.AP(tensor=ln_g.tensor, offset=0, ap=[[0, 128], [1, HEADS]])),
                (wo_nat[:, :, :], w_out.rearrange("d (k f) -> d k f", k=4)),
                (lnb[:, :], bass.AP(tensor=ln_b.tensor, offset=0, ap=[[0, 128], [1, HEADS]])),
                (b2_sb[:, :], b2), (rev[:, :, :], rev_dram),
            ]
            for h in range(HEADS):
                consts.append((mixw[IC * h:IC * h + IC, :],
                               bass.AP(tensor=reattn_w.tensor, offset=HEADS * h, ap=[[0, IC], [1, HEADS]])))
            assert len(first) == N_FIRST and len(consts) == N_CONSTS
            sp.dma_start(ident[:, :], ident_dram).then_inc(ident_loaded, 16)
            sp.wait_ge(xin_cleared, 1)
            load(0)
            for dst, src in first:
                sp.dma_start(dst, src).then_inc(first_loaded, 16)
            sp.dma_start(qkv[:, :, :], w_qkv.rearrange("(c p) d -> p c d", p=128)).then_inc(qkv_loaded, 16)
            for dst, src in consts:
                sp.dma_start(dst, src).then_inc(consts_loaded, 16)
            sp.dma_start(w1_sb[:, 0:E, :], w1.rearrange("e h f -> h e f")).then_inc(experts_loaded, 16)
            sp.dma_start(w1_sb[:, E, :], sw1).then_inc(experts_loaded, 16)
            sp.dma_start(w2_sb[:, 0:E, :], w2.rearrange("e f h -> f e h")).then_inc(experts_loaded, 16)
            sp.dma_start(w2_sb[:, E, :], sw2).then_inc(experts_loaded, 16)

            def do(step, G):
                if step == "XO" and exists(G + 2, NG):
                    wait_filled(sp, "XO", G)
                    load(G + 2)
                if step == "OT":
                    wait_emptied(sp, "OT", G)
                    sp.dma_start(out_rows[:, bass.ds(SLOTS * (G - 2), SLOTS), :],
                                 ostage[:, :, :]).then_inc(stored, 16)

            run(sp, do)
            sp.wait_ge(stored, 16 * NG)

        @block.tensor
        def _(pe):
            def fill(step, G=0):
                wait_free(pe, step, G)
                return bank(step)

            def transposes(step, G, pieces):
                for o, i, d in pieces:
                    last = pe.transpose(o, i, d)
                last.then_inc(filled[BANK[step]], 1)

            def prepare(step):
                if step.startswith("prep"):
                    return
                if step == "pT":
                    pe.wait_ge(first_loaded, 16 * N_FIRST)
                if step == "pA0":
                    pe.wait_ge(qkv_loaded, 16)
                if step == "pV":
                    pe.wait_ge(wv_g_ready, 1)
                if step == "pO":
                    pe.wait_ge(consts_loaded, 16 * N_CONSTS)
                if step == "pM":
                    wait_emptied(pe, "pO")
                ps = fill(step)
                columns = [ps[:, 128 * k:128 * k + 128] for k in range(4)]
                if step in ("pT", "pV", "pO"):
                    src = {"pT": tok_nat, "pV": wv_g, "pO": wo_nat}[step]
                    transposes(step, 0, [(columns[k], src[:, k, :], ident[:, :]) for k in range(4)])
                elif step in ("pA0", "pA1"):
                    half = int(step[2])
                    rows = slice(DH * half, DH * half + DH)
                    for k in range(4):
                        last = pe.matmul(columns[k], qkv[rows, k, :], qkv[rows, 4 + k, :], start=True, stop=True)
                    last.then_inc(filled[BANK[step]], 1)
                elif step == "pB":
                    transposes("pB", 0, [(ps[:, 0:12], vecs[:, :], ident[0:12, 0:12]),
                                         (ps[:, 16:24], gate_nat[:, :], ident[0:E, 0:E])])
                else:
                    for k in range(4):
                        last = pe.matmul(ps[:, 0:128], qkv[:, 8 + k, :], woTb[:, k, :], start=(k == 0), stop=(k == 3))
                    last.then_inc(filled[BANK["pM"]], 1)

            def attention(kind, b, s):
                if kind == "dots":
                    g = G_of[0]
                    wait_read(pe, g, [("Y6", 1), ("Y7", 1)])
                    pe.wait_ge(xT_ready, g + 1)
                    at_least(pe, exp_ready, b)
                    for c in range(CHUNKS):
                        o = NS * (c % HALF)
                        last = pe.matmul(ps_dots[:, c // HALF, o:o + NS],
                                         yT[:, 2 * s + c // HALF, c % HALF, :, :].rearrange("p h i -> p (h i)"),
                                         xT[:, N * s:N * s + NS], start=True, stop=True)
                    last.then_inc(dots_ready, 1)
                elif kind == "mix":
                    if isinstance(b, int) and b == 0:
                        pe.wait_ge(mixk_ready, 1)
                    pe.wait_ge(probs_ready, b + 1)
                    at_least(pe, aT_ready, b)
                    for c in range(CHUNKS):
                        o = 128 * (c % HALF)
                        last = pe.matmul(ps_mix[0:N, c // HALF, o:o + 128], probs[:, (s - 1) % 2, c, :],
                                         mixk[:, :, :].rearrange("p g i -> p (g i)"), start=True, stop=True)
                    last.then_inc(mix_ready, 1)
                else:
                    pe.wait_ge(aT_ready, b + 1)
                    at_least(pe, oT_ready, b)
                    for g in range(HEADS):
                        o = DH * (g % 2)
                        last = pe.matmul(ps_av[o:o + DH, NS * (g // 2):NS * (g // 2) + NS],
                                         v_sb[:, (s - 2) % SLOTS, DH * g:DH * g + DH], aT[:, s % 2, N * g:N * g + NS],
                                         start=True, stop=True)
                    last.then_inc(av_ready, 1)

            G_of = [0]

            def do(step, G):
                if isinstance(step, tuple):
                    kind, s = step
                    G_of[0] = G
                    if kind == "av":
                        vs = (s - 2) % SLOTS
                        wait_emptied(pe, f"V{vs}", G - 1)
                    if kind in ("dots", "mix", "av"):
                        attention(kind, SLOTS * G + s - BEHIND[kind], s)
                    return
                if step in NO_FILL:
                    return
                g = G + LAG[step]
                if isinstance(G, int) and G == FIRST:
                    for weight in {"TK": ["pT"], "Y0": ["pA0", "pA1"], "V0": ["pV"], "BS": ["pM"]}.get(step, []):
                        wait_emptied(pe, weight)
                if step == "XE":
                    if isinstance(G, int) and G == FIRST:
                        pe.wait_ge(pool_consts, 1)
                        pe.wait_ge(ident_loaded, 16)
                    pe.wait_ge(x_loaded, 16 * g + 16)
                if step == "BS":
                    pe.wait_ge(xsum_ready, g + 1)
                if step == "OP":
                    pe.wait_ge(oT_ready, SLOTS * g + SLOTS)
                if step == "CT":
                    pe.wait_ge(route, N_ROUTE * (g + 1))
                if step == "YF":
                    pe.wait_ge(units_ready, (E // 2 + 1) * (g + 1))
                if step == "RT" and isinstance(G, int):
                    pe.wait_ge(experts_loaded, 64)
                    pe.wait_ge(experts_ready, 3)
                operands = {
                    "TK": [("XE", 0), ("XO", 0)],
                    "TH": [("TK", 0)],
                    "TH2": [("OP", 0)],
                    "TX": [("TH", 0)],
                    "TX2": [("TH2", 0)],
                    "Y0": [("TX", 0)],
                    "V0": [("TX", 0)],
                    "RT": [("TX2", 0)],
                    "Z0": [("TX2", 1)],
                    "C0": [("CT", 1)],
                    "OT": [("YF", 0)],
                }
                wait_read(pe, G, operands.get(step, []), step)
                ps = bank(step)
                done = filled[BANK[step]]
                if step in ("XE", "XO"):
                    odd = 128 * (step == "XO")
                    transposes(step, G, [(ps[:, NS * s:NS * s + NS], xin[:, s, odd:odd + 128],
                                          ident[0:NS, 0:NS]) for s in range(SLOTS)])
                elif step == "TK":
                    for k in range(KT):
                        rows = [m[:, :, k // 2:k // 2 + N] for m in (xe, xo)[k % 2]]
                        last = products(ps[:, 0:W], [w[:, k, :] for w in tokT], rows, k == 0, k == KT - 1)
                    last.then_inc(done, 1)
                elif step in ("TH", "TH2"):
                    src = hT if step == "TH" else h2T
                    transposes(step, G, [(ps[0:N, 128 * s:128 * s + 128], src[:, s, :], ident[:, :])
                                         for s in range(SLOTS)])
                elif step in ("TX", "TX2"):
                    src = xn[step == "TX2"]
                    transposes(step, G, [(ps[:, N * s:N * s + NS], src[:, s, :], ident[0:NS, 0:NS])
                                         for s in range(SLOTS)])
                elif step[0] == "Y" and step != "YF":
                    products(ps[:, 0:W], [a[:, int(step[1]), :] for a in A], [m[:, 0:W] for m in xT_split])\
                        .then_inc(done, 1)
                elif step[0] == "V":
                    o = N * int(step[1])
                    products(ps[0:N, :], [m[:, o:o + N] for m in xT_split], [w[:, :, :] for w in wvT])\
                        .then_inc(done, 1)
                elif step == "BS":
                    pe.matmul(ps[:, 0:SLOTS], M[:, :], xsum[:, :], start=True, stop=True).then_inc(done, 1)
                elif step == "OP":
                    for k in range(4):
                        last = products(ps[:, 0:W], [w[:, k, :] for w in woT_split], [m[:, k, :, :] for m in oT],
                                        k == 0, k == 3)
                    last.then_inc(done, 1)
                elif step == "RT":
                    for s in range(SLOTS):
                        last = products(ps[0:N, E * s:E * s + E], [m[:, N * s:N * s + N] for m in x2T],
                                        [w[:, :] for w in gateT])
                    last.then_inc(done, 1)
                elif step == "CT":
                    transposes(step, G, [(ps[0:E, N * s:N * s + NS], combine[:, s, :], ident[0:NS, 0:NS])
                                         for s in range(SLOTS)])
                elif step[0] == "Z":
                    products(ps[:, 0:W], [w[:, int(step[1]), :] for w in w1_split], [m[:, :] for m in x2T])\
                        .then_inc(done, 1)
                elif step[0] == "C":
                    pe.matmul(ps[:, 0:W], pick[:, int(step[1]), :], combT[:, :], start=True, stop=True)\
                      .then_inc(done, 1)
                elif step == "YF":
                    pe.matmul(ps[:, 0:W], b2_both[:, :], combT[:, :], start=True, stop=False)
                    pe.matmul(ps[:, 0:W], b2_low[:, :], combT[0:E, :], start=False, stop=False)
                    for e in range(E + 1):
                        last = products(ps[:, 0:W], [w[:, e, :] for w in w2_split],
                                        [m[:, e, :] for m in act1_split], False, e == E)
                    last.then_inc(done, 1)
                elif step == "OT":
                    transposes(step, G, [(ps[0:N, 128 * s:128 * s + 128], fT[:, s, :], ident[:, :])
                                         for s in range(SLOTS)])

            run(pe, do, prepare)

        @block.scalar
        def _(act):
            def empty(step, G, dst, src, **kw):
                wait_filled(act, step, G)
                act.activation(dst, src, kw.pop("func", ACT.Copy), **kw).then_inc(emptied[BANK[step]], 1)

            def softmax_exp(b, s, half):
                if half == 0:
                    act.wait_ge(max_ready, b + 1)
                    at_least(act, probs_ready, b - 1)
                for c in range(HALF * half, HALF * half + HALF):
                    o = NS * (c % HALF)
                    last = act.activation(ex[:, s % 2, c, :], ps_dots[:, c // HALF, o:o + N],
                                          ACT.Exp, bias=negmax[:, c:c + 1], accum_out=sums[:, s % 2, c:c + 1])
                if half == 1:
                    last.then_inc(exp_ready, 1)

            def square(b):
                act.wait_ge(mix_ready, b + 1)
                at_least(act, sumsq_ready, b)
                act.activation(sq[:, :, :, :].rearrange("p (a c) g i -> p a (c g i)", a=2),
                               ps_mix[0:N, :, 0:128 * HALF], ACT.Square).then_inc(sq_ready, 1)

            def attention_rstd(b):
                act.wait_ge(sumsq_ready, b + 1)
                act.activation(lnvar[:, :, :], sumsq[:, :, :], ACT.Ln, bias=eps[0:N, 0:1], scale=1.0 / HEADS)\
                   .then_inc(lnvar_ready, 1)
                at_least(act, aT_ready, b)
                act.wait_ge(lnvar_ready, b + 1)
                act.activation(arstd[:, :, :], lnvar[:, :, :], ACT.Exp, scale=-0.5).then_inc(arstd_ready, 1)

            act.preload_act_table_set("natural_log_exp_and_others")
            act.wait_ge(pool_consts, 1)

            def prepare(step):
                if step in SPLIT_STEPS:
                    hi, _, scale = weight_parts(step)
                    wait_filled(act, step)
                    act.activation(hi, by4(bank(step)[:, :]), ACT.Copy, scale=scale).then_inc(weight_high, 1)
                if step == "pB":
                    wait_emptied(act, "pB")

            def do(step, G):
                if isinstance(step, tuple):
                    kind, s = step
                    b = SLOTS * G + s - BEHIND[kind]
                    if kind in ("exa", "exb"):
                        softmax_exp(b, s, int(kind == "exb"))
                    if kind == "ev":
                        act.wait_ge(av_ready, b + 1)
                        act.activation(oT[0][:, :, (s - 2) % SLOTS, :], values(), ACT.Copy).then_inc(oT_high, 1)
                    if kind == "sq":
                        square(b)
                    if kind == "rstd":
                        attention_rstd(b)
                    return
                g = G + LAG[step]
                if step == "R2":
                    act.wait_ge(route, N_ROUTE * g + 2)
                    act.activation(exl[:, :, :], shift_l[:, :, :], ACT.Exp).then_inc(exl_ready, 1)
                if step[0] == "H":
                    k = int(step[1])
                    last = f"C{2 * k + 1}" if k < E // 2 else f"Z{E}"
                    wait_emptied(act, last, G)
                    two = slice(2 * k, min(2 * k + 2, E + 1))
                    act.activation(act1_split[0][:, two, :], act1[:, two, :], ACT.Copy).then_inc(units_high, 1)
                if step in NO_FILL:
                    return
                ps = bank(step)
                if step in ("XE", "XO"):
                    wait_filled(act, step, G)
                    act.activation((xe if step == "XE" else xo)[0][:, :, :], patches(ps), ACT.Copy)\
                       .then_inc(patch_high, 1)
                elif step == "TK":
                    at_least(act, shifted, G + 1)
                    empty(step, G, hT[:, :, :].rearrange("p s n -> p (s n)"), ps[:, 0:W], func=ACT.Identity,
                          bias=vecT[:, 10:11])
                elif step == "TX":
                    wait_filled(act, step, G)
                    act.activation(xT_split[0][:, :], ps[:, 0:W], ACT.Copy).then_inc(high_ready[0], 1)
                elif step == "TX2":
                    wait_filled(act, step, G)
                    act.activation(x2T[0][:, :], ps[:, 0:W], ACT.Copy).then_inc(high_ready[1], 1)
                elif step == "CT":
                    wait_filled(act, step, G)
                    act.activation(combT[0:E, :], ps[0:E, 0:W], ACT.Copy).then_inc(high_ready[2], 1)
                elif step in ("Y0", "Y2", "Y4", "Y6"):
                    empty(step, G, yT[:, :, :, int(step[1]), :], chunked(ps))
                elif step in ("V0", "V2", "V3"):
                    empty(step, G, v_sb[:, int(step[1]), :], ps[0:N, :])
                elif step[0] == "Z":
                    e = int(step[1])
                    if e == 0:
                        at_least(act, units_ready, (E // 2 + 1) * g)
                        if present("YF", G - 1):
                            wait_filled(act, "YF", G - 1)
                    wait_filled(act, step, G)
                    ins = act.activation(act1[:, e, :], ps[:, 0:W], ACT.Relu, bias=vecT[:, e:e + 1])
                    ins.then_inc(emptied[BANK[step]], 1)
                elif step == "OT":
                    at_least(act, stored, 16 * g)
                    empty(step, G, ostage[:, :, :].rearrange("p s n -> p (s n)"), ps[0:N, :])

            run(act, do, prepare)

        @block.vector
        def _(dve):
            def empty(step, G, dst, src):
                wait_filled(dve, step, G)
                dve.tensor_copy(dst, src).then_inc(emptied[BANK[step]], 1)

            dve.wait_ge(pool_consts, 1)
            steps = [0]

            def halves(hi, lo, value):
                dve.tensor_copy(hi, value).then_inc(halved, 1)
                steps[0] += 1
                dve.wait_ge(halved, steps[0])
                return dve.tensor_tensor(lo, value, hi.bitcast(F32), ALU.subtract)

            def prepare(step):
                if step == "prepW":
                    dve.wait_ge(qkv_loaded, 16)
                    dve.wait_ge(consts_loaded, 16 * N_CONSTS)
                    for half in range(2):
                        rows = slice(DH * half, DH * half + DH)
                        last = dve.tensor_tensor(wv_g[rows, :, :], qkv[rows, 8:12, :],
                                                 lng[rows, half::2].unsqueeze(2).broadcast_to([DH, 4, 128]),
                                                 ALU.mult)
                    last.then_inc(wv_g_ready, 1)
                if step == "pO":
                    dve.wait_ge(weight_high, SPLIT_STEPS.index(step) + 1)
                    for half in range(2):
                        rows = slice(DH * half, DH * half + DH)
                        dve.tensor_tensor(woTb[rows, :, :], by4(bank(step)[rows, :]),
                                          lnb[rows, half::2].unsqueeze(2).broadcast_to([DH, 4, 128]), ALU.mult)
                if step in SPLIT_STEPS:
                    hi, lo, scale = weight_parts(step)
                    dve.wait_ge(weight_high, SPLIT_STEPS.index(step) + 1)
                    dve.scalar_tensor_tensor(out=lo, in0=by4(bank(step)[:, :]), scalar=scale, in1=hi.bitcast(F32),
                                             op0=ALU.mult, op1=ALU.subtract).then_inc(emptied[BANK[step]], 1)
                if step == "pB":
                    wait_filled(dve, "pB")
                    dve.tensor_copy(vecT[:, 0:12], bank("pB")[:, 0:12])
                    halves(gateT[0][:, :], gateT[1][:, :], bank("pB")[:, 16:24]).then_inc(emptied[BANK["pB"]], 1)
                if step == "pM":
                    wait_filled(dve, "pM")
                    dve.tensor_copy(M[:, :], bank("pM")[:, 0:128]).then_inc(emptied[BANK["pM"]], 1)
                if step == "prepX":
                    dve.tensor_reduce(mixmean[:, 0:1], mixw[:, :], AX_X, ALU.add).then_inc(prep, 1)
                    dve.tensor_reduce(diag16[:, :], ident[:, :].rearrange("p (h i) -> p i h", i=IC), AX_X, ALU.add)\
                       .then_inc(prep, 1)
                    dve.wait_ge(prep, 2)
                    dve.tensor_scalar(mixmean[:, 1:2], mixmean[:, 0:1], 1.0 / HEADS, None, ALU.mult).then_inc(prep, 1)
                    dve.wait_ge(prep, 3)
                    dve.tensor_scalar(mixc[:, :], mixw[:, :], mixmean[:, 1:2], None, ALU.subtract).then_inc(prep, 1)
                    dve.wait_ge(prep, 4)
                    dve.tensor_tensor(mixk[:, :, :], diag16[:, :].unsqueeze(1).broadcast_to([128, HEADS, IC]),
                                      mixc[:, :].unsqueeze(2).broadcast_to([128, HEADS, IC]), ALU.mult)\
                       .then_inc(mixk_ready, 1)
                if step == "prepE":
                    halves(b2_both[0:E, :], b2_low[:, :], b2_sb[:, :]).then_inc(halved, 1)
                    steps[0] += 1
                    dve.tensor_copy(b2_both[32:32 + E, :], b2_sb[:, :])
                    dve.tensor_tensor(pick[:, :, :], ident[0:64, 0:E].unsqueeze(2).broadcast_to([64, E, 128]),
                                      ident[0:64, 32:32 + E].unsqueeze(2).broadcast_to([64, E, 128]), ALU.add)\
                       .then_inc(experts_ready, 1)

            def norm_stats(k, step, G):
                g = G + LAG[step]
                ps = bank(step)
                wait_filled(dve, step, G)
                for s in range(SLOTS):
                    last = dve.bn_stats(stats[k][:, s, :], ps[0:N, 128 * s:128 * s + 128])
                last.then_inc(stats_ready[k], 1)
                dve.wait_ge(stats_ready[k], g + 1)
                dve.memset(scratch[:, :], 0.0)
                for s in range(SLOTS):
                    last = dve.bn_aggr(mv[k][:, s, :], stats[k][:, s, :])
                last.then_inc(mv_ready[k], 1)

            def norm_apply(k, step, G):
                g = G + LAG[step]
                ps = bank(step)
                dve.wait_ge(rstd_ready[k], g + 1)
                for s in range(SLOTS):
                    last = dve.tensor_scalar(xn[k][0:N, s, :], ps[0:N, 128 * s:128 * s + 128], mv[k][:, s, 0:1],
                                             rstd[k][:, s:s + 1], ALU.subtract, ALU.mult)
                last.then_inc(emptied[BANK[step]], 1)

            def routing(step, G):
                g = G + LAG[step]
                steps = [{"RT": 0, "R2": 2, "R3": 12}[step]]

                def link(ins):
                    steps[0] += 1
                    ins.then_inc(route, 1)
                    dve.wait_ge(route, N_ROUTE * g + steps[0])

                def wide(a):
                    return a.unsqueeze(2).broadcast_to([N, SLOTS, E])

                if step == "RT":
                    empty("RT", G, logit[:, :, :].rearrange("p s e -> p (s e)"), bank("RT")[0:N, 0:SLOTS * E])
                    wait_emptied(dve, "RT", G)
                    link(dve.tensor_reduce(top[:, 0, :], logit[:, :, :], AX_X, ALU.max))
                    link(dve.tensor_tensor(shift_l[:, :, :], logit[:, :, :], wide(top[:, 0, :]), ALU.subtract))
                elif step == "R2":
                    link(dve.scalar_tensor_tensor(out=key1[:, :, :], in0=shift_l[:, :, :], scalar=0.0, in1=rev[:, :, :],
                                                  op0=ALU.is_ge, op1=ALU.mult))
                    link(dve.tensor_reduce(top[:, 1, :], key1[:, :, :], AX_X, ALU.max))
                    link(dve.tensor_tensor(hot1[:, :, :], key1[:, :, :], wide(top[:, 1, :]), ALU.is_equal))
                    link(dve.scalar_tensor_tensor(out=rest[:, :, :], in0=hot1[:, :, :], scalar=-3e38,
                                                  in1=shift_l[:, :, :], op0=ALU.mult, op1=ALU.add))
                    link(dve.tensor_reduce(top[:, 2, :], rest[:, :, :], AX_X, ALU.max))
                    link(dve.tensor_tensor(key1[:, :, :], rest[:, :, :], wide(top[:, 2, :]), ALU.is_equal))
                    link(dve.tensor_tensor(key2[:, :, :], key1[:, :, :], rev[:, :, :], ALU.mult))
                    link(dve.tensor_reduce(top[:, 3, :], key2[:, :, :], AX_X, ALU.max))
                    link(dve.tensor_tensor(hot2[:, :, :], key2[:, :, :], wide(top[:, 3, :]), ALU.is_equal))
                    link(dve.tensor_tensor(hot1[:, :, :], hot1[:, :, :], hot2[:, :, :], ALU.add))
                else:
                    dve.wait_ge(exl_ready, g + 1)
                    link(dve.tensor_reduce(top[:, 4, :], exl[:, :, :], AX_X, ALU.add))
                    link(dve.tensor_tensor(key1[:, :, :], exl[:, :, :], hot1[:, :, :], ALU.mult))
                    link(dve.tensor_reduce(top[:, 5, :], key1[:, :, :], AX_X, ALU.add))
                    link(dve.scalar_tensor_tensor(out=top[:, 6, :], in0=top[:, 4, :], scalar=1e-20, in1=top[:, 5, :],
                                                  op0=ALU.mult, op1=ALU.add))
                    link(dve.reciprocal(top[:, 7, :], top[:, 6, :]))
                    link(dve.tensor_tensor(combine[0:N, :, :], key1[:, :, :], wide(top[:, 7, :]), ALU.mult))
                assert steps[0] == {"RT": 2, "R2": 12, "R3": N_ROUTE}[step]

            def scores_max(b):
                dve.wait_ge(dots_ready, b + 1)
                at_least(dve, exp_ready, b)
                scores = ps_dots[:, :, 0:HALF * NS].rearrange("p a (c j) -> p a c j", c=HALF)
                dve.tensor_reduce(negmax[:, :].rearrange("p (a c) -> p a c", a=2),
                                  scores[:, :, :, 0:N], AX_X, ALU.max, negate=True).then_inc(max_ready, 1)

            def invert_sums(b, s):
                dve.wait_ge(exp_ready, b + 1)
                at_least(dve, probs_ready, b - 1)
                dve.reciprocal(rinv[:, s % 2, :], sums[:, s % 2, :]).then_inc(rinv_ready, 1)

            def scale_mixed(b, s):
                dve.wait_ge(arstd_ready, b + 1)
                at_least(dve, av_ready, b - 1)
                to = aT[:, (s - 1) % 2, 0:HEADS * N].rearrange("p (g n) -> p g n", n=N)
                mixed = ps_mix[0:N, :, 0:128 * HALF].rearrange("p a (c g i) -> p a c g i", c=HALF, g=HEADS)
                scale = arstd[:, :, :].rearrange("p (a c) i -> p a c i", a=2)
                row = STARTS[1]
                for a in range(2):
                    dst = bass.AP(tensor=to.tensor, offset=to.offset + STARTS[HALF * a],
                                  ap=[list(to.ap[0]), [row, HALF], [N, HEADS], [1, row]])
                    dve.tensor_tensor(dst, mixed[:, a, :, :, 0:row],
                                      scale[:, a, :, 0:row].unsqueeze(2).broadcast_to([N, HALF, HEADS, row]), ALU.mult)
                dve.tensor_tensor(to[:, :, STARTS[HALF] - 1::STARTS[HALF]].rearrange("p g a -> p a g"),
                                  mixed[:, :, HALF - 1, :, row],
                                  scale[:, :, HALF - 1, row].unsqueeze(2).broadcast_to([N, 2, HEADS]), ALU.mult)\
                   .then_inc(aT_ready, 1)

            def do(step, G):
                if isinstance(step, tuple):
                    kind, s = step
                    b = SLOTS * G + s - BEHIND[kind]
                    if kind == "max":
                        scores_max(b)
                    if kind == "inv":
                        invert_sums(b, s)
                    if kind == "scale":
                        scale_mixed(b, s)
                    if kind == "ev":
                        dve.wait_ge(oT_high, b + 1)
                        hi, lo = [m[:, :, (s - 2) % SLOTS, :] for m in oT]
                        dve.tensor_tensor(lo, values(), hi.bitcast(F32), ALU.subtract).then_inc(oT_ready, 1)
                    return
                if step in ("RT", "R2", "R3"):
                    routing(step, G)
                if step[0] == "H" and step not in UNITS_BY_POOL:
                    low_units(dve, step, G)
                if step == "XS":
                    dve.wait_ge(xT_ready, G + LAG[step] + 1)
                    dve.tensor_reduce(xsum[:, :], xT[:, 0:W].rearrange("p (s n) -> p s n", n=N), AX_X, ALU.add)\
                       .then_inc(xsum_ready, 1)
                if step in ("NH", "NH2"):
                    k = int(step == "NH2")
                    norm_apply(k, ("TH", "TH2")[k], G)
                if step in NO_FILL:
                    return
                g = G + LAG[step]
                ps = bank(step)
                if step in ("Y1", "Y3", "Y5", "Y7"):
                    empty(step, G, yT[:, :, :, int(step[1]), :], chunked(ps))
                elif step in ("XE", "XO"):
                    dve.wait_ge(patch_high, 2 * g + 1 + (step == "XO"))
                    hi, lo = [m[:, :, :] for m in (xe if step == "XE" else xo)]
                    dve.tensor_tensor(lo, patches(ps), hi.bitcast(F32), ALU.subtract)\
                       .then_inc(emptied[BANK[step]], 1)
                elif step == "V1":
                    empty(step, G, v_sb[:, 1, :], ps[0:N, :])
                elif step in ("TH", "TH2"):
                    norm_stats(int(step == "TH2"), step, G)
                elif step == "OP":
                    wait_emptied(dve, "YF", G)
                    at_least(dve, shifted, G)
                    wait_filled(dve, step, G)
                    for s in range(SLOTS):
                        last = dve.scalar_tensor_tensor(out=h2T[:, s, :], in0=ps[:, N * s:N * s + N],
                                                        scalar=bias_old[:, s:s + 1], in1=hT_old[:, s, :],
                                                        op0=ALU.add, op1=ALU.add)
                    last.then_inc(emptied[BANK[step]], 1)
                elif step in ("TX", "TX2"):
                    hi, lo = xT_split if step == "TX" else x2T
                    dve.wait_ge(high_ready[int(step == "TX2")], g + 1)
                    dve.tensor_tensor(lo[:, :], ps[:, 0:W], hi[:, :].bitcast(F32), ALU.subtract)\
                       .then_inc(emptied[BANK[step]], 1)
                elif step == "BS":
                    at_least(dve, shifted, G + 1)
                    if isinstance(G, int) and G == FIRST:
                        wait_emptied(dve, "pB")
                    wait_filled(dve, step, G)
                    dve.tensor_scalar(bias[:, :], ps[:, 0:SLOTS], vecT[:, 11:12], None, ALU.add)\
                       .then_inc(emptied[BANK[step]], 1)
                elif step == "CT":
                    dve.wait_ge(high_ready[2], g + 1)
                    dve.tensor_tensor(combT[32:32 + E, :], ps[0:E, 0:W], combT[0:E, :].bitcast(F32), ALU.subtract)\
                       .then_inc(emptied[BANK[step]], 1)
                elif step[0] == "C":
                    e = int(step[1])
                    wait_filled(dve, step, G)
                    wait_emptied(dve, f"Z{e}", G)
                    ins = dve.tensor_tensor(act1[:, e, :], ps[:, 0:W], act1[:, e, :], ALU.mult)
                    ins.then_inc(emptied[BANK[step]], 1)
                elif step == "YF":
                    wait_filled(dve, step, G)
                    dve.scalar_tensor_tensor(out=fT[:, :, :].rearrange("p s n -> p (s n)"), in0=ps[:, 0:W],
                                             scalar=vecT[:, 9:10], in1=h2T[:, :, :].rearrange("p s n -> p (s n)"),
                                             op0=ALU.add, op1=ALU.add).then_inc(emptied[BANK[step]], 1)

            run(dve, do, prepare)

        @block.gpsimd
        def _(pool):
            pool.memset(xin[:, :, :], 0.0).then_inc(xin_cleared, 1)
            pool.memset(minus_half[:, :], -0.5)
            for tile in xn:
                pool.memset(tile[:, :, :], 0.0)
            pool.memset(combine[:, :, :], 0.0)
            pool.memset(combT[:, :].bitcast(F32), 0.0)
            pool.memset(b2_both[:, :].bitcast(F32), 0.0)
            pool.memset(xT[:, W:], 0.0)
            pool.memset(aT[:, :, HEADS * N:], 0.0)
            pool.memset(ones[:, :], 1.0)
            pool.memset(eps[:, :], LN_EPS).then_inc(pool_consts, 1)
            pool.wait_ge(pool_consts, 1)

            def prepare(step):
                if step == "prepE":
                    pool.wait_ge(experts_loaded, 64)
                    for n, ((hi, lo), raw) in enumerate([(w1_split, w1_sb), (w2_split, w2_sb)]):
                        pool.tensor_scalar(hi[:, :, :], raw, 1.0, 0.0, ALU.mult, ALU.add).then_inc(experts_high, 1)
                        pool.wait_ge(experts_high, n + 1)
                        pool.tensor_tensor(lo[:, :, :], raw, hi[:, :, :].bitcast(F32), ALU.subtract)\
                            .then_inc(experts_ready, 1)

            def do(step, G):
                if isinstance(step, tuple):
                    kind, s = step
                    b = SLOTS * G + s - BEHIND[kind]
                    if kind == "inv":
                        pool.wait_ge(rinv_ready, b + 1)
                        at_least(pool, mix_ready, b - 1)
                        pool.tensor_tensor(probs[:, s % 2, :, :], ex[:, s % 2, :, :],
                                           rinv[:, s % 2, :].unsqueeze(2).broadcast_to([128, CHUNKS, N]),
                                           ALU.mult).then_inc(probs_ready, 1)
                    if kind == "sq":
                        pool.wait_ge(sq_ready, b + 1)
                        pool.tensor_tensor(sum4[:, :, :, :], sq[:, :, 0:4, :], sq[:, :, 4:8, :], ALU.add)\
                            .then_inc(tree4, 1)
                        pool.wait_ge(tree4, b + 1)
                        pool.tensor_tensor(sum2[:, :, :, :], sum4[:, :, 0:2, :], sum4[:, :, 2:4, :], ALU.add)\
                            .then_inc(tree2, 1)
                        pool.wait_ge(tree2, b + 1)
                        at_least(pool, lnvar_ready, b)
                        pool.tensor_tensor(sumsq[:, :, :], sum2[:, :, 0, :], sum2[:, :, 1, :], ALU.add)\
                            .then_inc(sumsq_ready, 1)
                    return
                if step == "XS":
                    g = G + LAG[step]
                    wait_emptied(pool, "TX", G)
                    at_least(pool, xsum_ready, g)
                    hi, lo = [m[:, :].bitcast(F32) for m in xT_split]
                    pool.tensor_tensor(xT[:, 0:W], hi, lo, ALU.add).then_inc(xT_ready, 1)
                if step in UNITS_BY_POOL:
                    low_units(pool, step, G)
                if step in ("NH", "NH2"):
                    k = int(step == "NH2")
                    g = G + LAG[step]
                    pool.wait_ge(mv_ready[k], g + 1)
                    pool.tensor_tensor(vare[k][:, :], mv[k][:, :, 1], eps[0:N, :], ALU.add)\
                        .then_inc(vare_ready[k], 1)
                    pool.wait_ge(vare_ready[k], g + 1)
                    pool.tensor_tensor(rstd[k][:, :], vare[k][:, :], minus_half[0:N, :], ALU.pow)\
                        .then_inc(rstd_ready[k], 1)
                if step == "shift":
                    wait_read(pool, G, [("OP", 0), ("TK", 1), ("BS", 1)])
                    pool.tensor_tensor(bias_old[:, :], bias[:, :], ones[:, :], ALU.mult)
                    pool.tensor_copy(hT_old[:, :, :], hT[:, :, :]).then_inc(shifted, 1)

            run(pool, do, prepare)


_INS = ['x', 'L0_tok_W', 'L0_tok_b', 'L0_attn_w_qkv', 'L0_attn_reattn_w', 'L0_attn_ln_g', 'L0_attn_ln_b',
        'L0_attn_w_out', 'L0_attn_b_out', 'L0_ffn_gate_w', 'L0_ffn_w1', 'L0_ffn_b1', 'L0_ffn_w2', 'L0_ffn_b2',
        'L0_ffn_sw1', 'L0_ffn_sb1', 'L0_ffn_sw2', 'L0_ffn_sb2']


def kernel(**inputs):
    import concourse.bacc as _bacc
    from concourse.bass_utils import run_bass_kernel_spmd as _run

    nc = _bacc.Bacc("TRN2", target_bir_lowering=False, num_devices=1)
    arrays, args = {}, []
    for name in _INS:
        a = np.ascontiguousarray(inputs[name])
        arrays[f"in_{name}"] = a
        args.append(nc.dram_tensor(f"in_{name}", a.shape, mybir.dt.from_np(a.dtype), kind="ExternalInput").ap())
    consts = {"ident": np.eye(128, dtype=np.float32),
              "rev": np.broadcast_to(np.arange(E, 0, -1, dtype=np.float32), (N, SLOTS, E)).copy()}
    for name, a in consts.items():
        arrays[f"const_{name}"] = a
        args.append(nc.dram_tensor(f"const_{name}", a.shape, F32, kind="ExternalInput").ap())
    args.append(nc.dram_tensor("out_0", (B, N, D), F32, kind="ExternalOutput").ap())
    audio_tower(nc, *args)
    r = _run(nc, [arrays], core_ids=[0])
    return r.results[0]["out_0"]
```
